# Optimizing a Trainium2 kernel written in Bass

```python
import numpy as np
import jax
import jax.numpy as jnp

def _softmax(x, axis=-1):
    return jax.nn.softmax(x, axis=axis)

def _gelu(x):
    return jax.nn.gelu(x, approximate=True)

def _silu(x):
    return jax.nn.silu(x)

def _sigmoid(x):
    return jax.nn.sigmoid(x)

def _layernorm(x, axis=-1, eps=1e-05):
    m = jnp.mean(x, axis=axis, keepdims=True)
    v = jnp.var(x, axis=axis, keepdims=True)
    return (x - m) / jnp.sqrt(v + eps)

def _scatter_add(tgt, idx, src, axis=0):
    return tgt.at[idx].add(src)

def _segment_sum(src, seg, n):
    return jax.ops.segment_sum(src, seg, n)
kernel_name = 'mk_adj_resnorm_d2_adj_r2_8bcbf5'

def setup_inputs(seed: int=0):
    np.random.seed(seed)
    _w = jnp.asarray

    def _rec_inputs():
        import jax
        import jax.numpy as jnp
        _gk = jax.random.key(seed)
        x = -0.003407 + 1.001 * jax.random.normal(jax.random.fold_in(_gk, 1), (512, 128), jnp.float32)
        _w = (1.0 + jnp.arange(512, dtype=jnp.float32)) ** (-0.5)
        _w = _w / _w.mean()
        _pij = jnp.clip(0.00390625 * _w[:, None] * _w[None, :], 0.0, 1.0)
        _a = jax.random.uniform(jax.random.fold_in(_gk, 2), (512, 512)) < _pij
        adj = _a.astype(jnp.int32)
        return (x, adj)
    x, adj = _rec_inputs()

    def _L0_gnn_setup():
        import jax, jax.numpy as jnp
        import numpy as np
        N = 512
        H = 128
        key = jax.random.key(seed)
        k1, k2, k3, k4, k5, k6, k7 = jax.random.split(key, 7)
        s = 1.0 / np.sqrt(H)
        node_features = jax.random.normal(k1, (N, H), dtype=jnp.float32)
        adjacency_matrix = jax.random.randint(k2, (N, N), 0, 2, dtype=jnp.int32)
        edge_table = jax.random.normal(k3, (N * N, H), dtype=jnp.float32)
        w_ih = jax.random.uniform(k4, (3 * H, H), minval=-s, maxval=s, dtype=jnp.float32)
        w_hh = jax.random.uniform(k5, (3 * H, H), minval=-s, maxval=s, dtype=jnp.float32)
        b_ih = jax.random.uniform(k6, (3 * H,), minval=-s, maxval=s, dtype=jnp.float32)
        b_hh = jax.random.uniform(k7, (3 * H,), minval=-s, maxval=s, dtype=jnp.float32)
        return {'node_features': node_features, 'adjacency_matrix': adjacency_matrix, 'edge_table': edge_table, 'w_ih': w_ih, 'w_hh': w_hh, 'b_ih': b_ih, 'b_hh': b_hh}
    _L0_gnn_all = _L0_gnn_setup()
    _L0_gnn_in = {k: v for k, v in _L0_gnn_all.items() if k in ('edge_table', 'w_ih', 'w_hh', 'b_ih', 'b_hh')}
    del _L0_gnn_all

    def _L1_gnn_setup():
        import jax, jax.numpy as jnp
        import numpy as np
        NUM_NODES = 3072
        INPUT_DIM = 128
        OUTPUT_DIM = 128
        NUM_HEADS = 4
        HEAD_DIM = OUTPUT_DIM // NUM_HEADS
        NEG_INF = -9000000000000000.0
        key = jax.random.key(seed)
        k_x, k_adj, k_W, k_a = jax.random.split(key, 4)
        x = jax.random.normal(k_x, (NUM_NODES, INPUT_DIM), dtype=jnp.float32)
        adj = jax.random.randint(k_adj, (NUM_NODES, NUM_NODES), 0, 2, dtype=jnp.int32)
        W = jax.random.uniform(k_W, (NUM_HEADS, INPUT_DIM, HEAD_DIM), dtype=jnp.float32, minval=-1.0, maxval=1.0) * np.sqrt(6.0 / INPUT_DIM)
        a = jax.random.uniform(k_a, (NUM_HEADS, 2 * HEAD_DIM, 1), dtype=jnp.float32, minval=-1.0, maxval=1.0) * np.sqrt(6.0 / (2 * HEAD_DIM))
        return {'x': x, 'adj': adj, 'W': W, 'a': a}
    _L1_gnn_all = _L1_gnn_setup()
    _L1_gnn_in = {k: v for k, v in _L1_gnn_all.items() if k in ('W', 'a')}
    del _L1_gnn_all
    return {'x': x, 'adj': adj, 'L0_gnn_edge_table': _L0_gnn_in['edge_table'], 'L0_gnn_w_ih': _L0_gnn_in['w_ih'], 'L0_gnn_w_hh': _L0_gnn_in['w_hh'], 'L0_gnn_b_ih': _L0_gnn_in['b_ih'], 'L0_gnn_b_hh': _L0_gnn_in['b_hh'], 'L1_gnn_W': _L1_gnn_in['W'], 'L1_gnn_a': _L1_gnn_in['a']}

def reference(x, adj, L0_gnn_edge_table, L0_gnn_w_ih, L0_gnn_w_hh, L0_gnn_b_ih, L0_gnn_b_hh, L1_gnn_W, L1_gnn_a):
    import jax
    import jax.numpy as jnp

    def _L0_gnn_ref(node_features, adjacency_matrix, edge_table, w_ih, w_hh, b_ih, b_hh):
        import jax, jax.numpy as jnp
        import numpy as np
        N = 512
        H = 128
        n, h = node_features.shape
        T = edge_table.reshape(n, n, h)
        adj = adjacency_matrix.astype(node_features.dtype)
        agg = jnp.einsum('ij,jh,ijh->ih', adj, node_features, T)
        gi = agg @ w_ih.T + b_ih
        gh = node_features @ w_hh.T + b_hh
        ir, iz, in_ = jnp.split(gi, 3, axis=-1)
        hr, hz, hn = jnp.split(gh, 3, axis=-1)
        r = jax.nn.sigmoid(ir + hr)
        z = jax.nn.sigmoid(iz + hz)
        nn_ = jnp.tanh(in_ + r * hn)
        return (1.0 - z) * nn_ + z * node_features

    def _L1_gnn_ref(x, adj, W, a):
        import jax, jax.numpy as jnp
        import numpy as np
        NUM_NODES = 3072
        INPUT_DIM = 128
        OUTPUT_DIM = 128
        NUM_HEADS = 4
        HEAD_DIM = OUTPUT_DIM // NUM_HEADS
        NEG_INF = -9000000000000000.0
        H, Din, d = W.shape
        N = x.shape[0]
        h = jnp.einsum('ni,hid->hnd', x, W)
        a_dst = a[:, :d, 0]
        a_src = a[:, d:, 0]
        s_dst = jnp.einsum('hnd,hd->hn', h, a_dst)
        s_src = jnp.einsum('hnd,hd->hn', h, a_src)
        energy = jax.nn.leaky_relu(s_src[:, :, None] + s_dst[:, None, :], negative_slope=0.2)
        energy = jnp.where(adj[None] > 0, energy, NEG_INF)
        attention = jax.nn.softmax(energy, axis=-1)
        h_prime = jnp.einsum('hij,hjd->hid', attention, h)
        return jnp.reshape(h_prime, (N, H * d))
    x = _layernorm(x + _L0_gnn_ref(x, adj, L0_gnn_edge_table, L0_gnn_w_ih, L0_gnn_w_hh, L0_gnn_b_ih, L0_gnn_b_hh), axis=-1)
    x = _layernorm(x + _L1_gnn_ref(x, adj, L1_gnn_W, L1_gnn_a), axis=-1)
    return x

_drawn_inputs = setup_inputs


def setup_inputs(seed=0):
    import zlib

    import numpy as np

    out = dict(_drawn_inputs(seed))
    spreads = {}
    factors = {'L0_gnn_b_ih': 2.838, 'L0_gnn_b_hh': 4.706}
    for name, (base, spread) in spreads.items():
        noise = np.random.default_rng([zlib.crc32(name.encode()), seed]).standard_normal(out[name].shape)
        drawn = base * np.exp(spread * noise) if base else spread * noise
        out[name] = jnp.asarray(drawn.astype(out[name].dtype))
    for name, factor in factors.items():
        out[name] = (out[name] * factor).astype(out[name].dtype)
    return out
```

```python
from contextlib import ExitStack

import concourse.bass as bass
from concourse import mybir

F32 = mybir.dt.float32
I32 = mybir.dt.int32
ALU = mybir.AluOpType
ACT = mybir.ActivationFunctionType

P = 128
EPS = 1e-5
SLOPE = 0.2
NEG = -1e30


def build_gnn(nc, x, adj, edge_table, w_ih, w_hh, b_ih, b_hh, w_gat, a_gat, out):
    N, H = x.shape
    Q = N // P
    NH, _, D = w_gat.shape
    G = 4
    NBUF = 4
    NGROUP = N // G
    assert H == P and NH * D == H and Q == 4

    with ExitStack() as ctx:
        def sb(name, shape, dt=F32):
            return ctx.enter_context(nc.sbuf_tensor(name, shape, dt))

        def ps(name, shape, dt=F32):
            return ctx.enter_context(nc.psum_tensor(name, shape, dt))

        def sem(name):
            return ctx.enter_context(nc.semaphore(name))

        x_sb = sb("x_sb", [P, Q, H])
        x_il = sb("x_il", [P, Q, H])
        adj_i = sb("adj_i", [P, Q, N], I32)
        wih_sb = sb("wih_sb", [P, 3, H])
        whh_sb = sb("whh_sb", [P, 3, H])
        bias_in = sb("bias_in", [1, 2, 3, H])
        wg_sb = sb("wg_sb", [P, NH, D])
        a_col = sb("a_col", [P, 2])
        ident = sb("ident", [P, P])
        ones_row = sb("ones_row", [1, P])
        bias_row = sb("bias_row", [1, 4, Q, H])
        headmask = sb("headmask", [P, NH])
        adj_f = sb("adj_f", [P, Q, N])
        negm = sb("negm", [P, Q, N])
        adjT = sb("adjT", [P, Q, N])
        xT = sb("xT", [P, Q, P])
        wT = sb("wT", [P, 7, P])
        a_bd = sb("a_bd", [P, 2, NH])
        wa = sb("wa", [P, 2 * NH])
        wa_wide = sb("wa_wide", [P, NH, P])
        T_buf = sb("T_buf", [P, NBUF, G, Q * H])
        prod = sb("prod", [P, 2, G, Q * H])
        acol = sb("acol", [P, 2, Q, Q])
        aggT = sb("aggT", [P, Q, P])
        g_r = sb("g_r", [P, Q, H])
        g_z = sb("g_z", [P, Q, H])
        g_n = sb("g_n", [P, Q, H])
        g_t = sb("g_t", [P, Q, H])
        y = sb("y", [P, Q, H])
        st6 = sb("st6", [P, Q, 6])
        mv = sb("mv", [P, Q, 2])
        epsv = sb("epsv", [P, Q])
        mhalf = sb("mhalf", [P, Q])
        rstd = sb("rstd", [P, Q])
        x1 = sb("x1", [P, Q, H])
        x1T = sb("x1T", [P, Q, P])
        x1T_il = x1T[:].rearrange("h t p -> h (t p)").rearrange("h (s q) -> h q s", q=Q)
        h_sb = sb("h_sb", [P, Q, H])
        u_sb = sb("u_sb", [P, Q, 2 * NH])
        vm = sb("vm", [P, NH, N])
        vmax = sb("vmax", [P, NH])
        m1 = sb("m1", [P, NH])
        nmax = sb("nmax", [P, NH])
        e_sb = sb("e_sb", [P, NH, N])
        p_sb = sb("p_sb", [P, NH, N])
        rsum = sb("rsum", [P, NH])
        rinv = sb("rinv", [P, NH])
        pT = sb("pT", [P, NH, Q, P])
        hp = sb("hp", [P, Q, H])
        out_sb = sb("out_sb", [P, Q, H])

        ps_gate = [ps(f"ps_gate{k}", [P, Q, H]) for k in range(4)]
        ps_v = ps_gate
        ps_t = [ps(f"ps_t{k}", [P, 4, P]) for k in range(2)]
        ps_a = ps("ps_a", [P, Q, P])
        ps_b = ps("ps_b", [P, 512])
        ps_ab = [ps_a[:].rearrange("p q i -> p (q i)"), ps_b[:]]

        s_x = sem("s_x"); s_xi = sem("s_xi"); s_adj = sem("s_adj"); s_w = sem("s_w"); s_bias = sem("s_bias"); s_ac = sem("s_ac")
        s_T = [sem(f"s_T{b}") for b in range(NBUF)]
        s_const = sem("s_const"); s_biasrow = sem("s_biasrow"); s_abd = sem("s_abd")
        s_wide = sem("s_wide"); s_wa = sem("s_wa"); s_wacp = sem("s_wacp")
        s_adjf = sem("s_adjf"); s_neg = sem("s_neg")
        s_tp = sem("s_tp"); s_tc = sem("s_tc")
        s_prod = sem("s_prod"); s_acol = sem("s_acol"); s_agg = sem("s_agg"); s_aggc = sem("s_aggc")
        s_gate = sem("s_gate"); s_rz = sem("s_rz"); s_dv = sem("s_dv"); s_nn = sem("s_nn"); s_npre = sem("s_npre")
        s_var = sem("s_var"); s_rstd = sem("s_rstd"); s_x1 = sem("s_x1")
        s_h = sem("s_h"); s_hc = sem("s_hc"); s_v = sem("s_v")
        s_e = sem("s_e"); s_p = sem("s_p"); s_pt = sem("s_pt"); s_ptc = sem("s_ptc"); s_att = sem("s_att")
        s_o = sem("s_o"); s_out = sem("s_out")

        x_v = x.rearrange("(p q) h -> p q h", q=Q)
        out_v = out.rearrange("(t p) h -> p t h", p=P)
        adj_v = adj.rearrange("(p q) j -> p q j", q=Q)
        T_v = edge_table.rearrange("(i p q) h -> i p (q h)", p=P, q=Q)

        block = ctx.enter_context(nc.Block())

        @block.sync
        def _(sp):
            sp.dma_start(x_sb[:], x.rearrange("(t p) h -> p t h", p=P)).then_inc(s_x, 16)
            sp.dma_start(x_il[:], x_v).then_inc(s_xi, 16)
            sp.dma_start(adj_i[:], adj_v).then_inc(s_adj, 16)
            sp.dma_start(wih_sb[:], w_ih.rearrange("(g p) h -> p g h", p=P)).then_inc(s_w, 16)
            sp.dma_start(whh_sb[:], w_hh.rearrange("(g p) h -> p g h", p=P)).then_inc(s_w, 16)
            sp.dma_start(wg_sb[:], w_gat.rearrange("n p d -> p n d")).then_inc(s_w, 16)
            sp.dma_start(bias_in[:, 0], b_ih.rearrange("(a g h) -> a g h", a=1, g=3)).then_inc(s_bias, 16)
            sp.dma_start(bias_in[:, 1], b_hh.rearrange("(a g h) -> a g h", a=1, g=3)).then_inc(s_bias, 16)
            with nc.allow_non_contiguous_dma(reason="256 attention weights"):
                for n in range(NH):
                    sp.dma_start(a_col[n * D:(n + 1) * D, :],
                                 a_gat[n, :, 0].rearrange("(k d) -> d k", k=2)).then_inc(s_ac, 16)
            for b in range(NBUF):
                sp.dma_start(T_buf[:, b], T_v[b * G:(b + 1) * G].rearrange("i p f -> p i f")).then_inc(s_T[b], 16)
            with sp.Fori(0, NGROUP // NBUF - 1) as it:
                for b in range(NBUF):
                    sp.wait_ge(s_prod, it * NBUF + b + 1)
                    src = T_v[bass.ds((it * NBUF + b + NBUF) * G, G)].rearrange("i p f -> p i f")
                    sp.dma_start(T_buf[:, b], src).then_inc(s_T[b], 16)
            sp.wait_ge(s_o, 1)
            sp.dma_start(out_v, out_sb[:]).then_inc(s_out, 16)
            sp.wait_ge(s_out, 16)

        @block.gpsimd
        def _(pool):
            nc.gpsimd.memset(ident[:], 0.0).then_inc(s_const, 1)
            nc.gpsimd.memset(headmask[:], 1.0).then_inc(s_const, 1)
            nc.gpsimd.memset(mhalf[:], -0.5).then_inc(s_const, 1)
            nc.gpsimd.memset(ones_row[:], 1.0).then_inc(s_const, 1)
            pool.wait_ge(s_const, 4)
            nc.gpsimd.affine_select(out=ident[:], in_=ident[:], compare_op=ALU.not_equal, fill=1.0, base=0,
                                    pattern=[[-1, P]], channel_multiplier=1).then_inc(s_const, 1)
            nc.gpsimd.affine_select(out=headmask[:], in_=headmask[:], compare_op=ALU.is_ge, fill=0.0, base=0,
                                    pattern=[[-D, NH]], channel_multiplier=1).then_inc(s_const, 1)
            pool.wait_ge(s_const, 6)
            nc.gpsimd.affine_select(out=headmask[:], in_=headmask[:], compare_op=ALU.is_ge, fill=0.0, base=D - 1,
                                    pattern=[[D, NH]], channel_multiplier=-1).then_inc(s_const, 1)
            pool.wait_ge(s_tc, 7)
            with pool.Fori(0, NGROUP // 2) as it:
                for par in range(2):
                    pool.wait_ge(s_agg, it * 2)
                    src = adjT[:].rearrange("p j (q i) -> p j q i", q=Q)[:, :, :, bass.ds(it * 2 + par, 1)]
                    nc.gpsimd.tensor_copy(acol[:, par].unsqueeze(3), src).then_inc(s_acol, 1)
            for k in range(2):
                pool.wait_ge(s_var, k + 1)
                nc.gpsimd.tensor_tensor(rstd[:], epsv[:], mhalf[:], ALU.pow).then_inc(s_rstd, 1)

        @block.scalar
        def _(act):
            for k in range(2):
                act.wait_ge(s_tp, k + 1)
                dst = xT[:] if k == 0 else wT[:, 0:4]
                nc.scalar.copy(dst, ps_t[k][:]).then_inc(s_tc, 1)
            act.wait_ge(s_tp, 3)
            nc.scalar.copy(wT[:, 4:7], ps_t[0][:, 0:3]).then_inc(s_tc, 1)
            for j in range(Q):
                act.wait_ge(s_tp, 4 + j)
                nc.scalar.copy(adjT[:, j], ps_t[(3 + j) % 2][:].rearrange("p q i -> p (q i)")).then_inc(s_tc, 1)
            act.wait_ge(s_wa, 1)
            nc.scalar.copy(wa[:], ps_b[:, 0:2 * NH]).then_inc(s_wacp, 1)
            with act.Fori(0, NGROUP // 2) as it:
                for par in range(2):
                    act.wait_ge(s_agg, it * 2 + par + 1)
                    dst = aggT[:].rearrange("h t p -> h (t p)")[:, bass.ds((it * 2 + par) * G, G)]
                    nc.scalar.copy(dst, ps_ab[par][:, 0:G]).then_inc(s_aggc, 1)
            act.wait_ge(s_gate, 1)
            nc.scalar.activation(g_r[:], ps_gate[0][:], ACT.Tanh, scale=0.5).then_inc(s_rz, 1)
            nc.scalar.activation(g_z[:], ps_gate[1][:], ACT.Tanh, scale=0.5).then_inc(s_rz, 1)
            act.wait_ge(s_npre, 1)
            nc.scalar.activation(g_n[:], g_n[:], ACT.Tanh).then_inc(s_nn, 1)
            act.wait_ge(s_h, 1)
            nc.scalar.copy(x1T[:], ps_t[0][:]).then_inc(s_hc, 1)
            act.wait_ge(s_h, 2)
            nc.scalar.copy(h_sb[:], ps_a[:]).then_inc(s_hc, 1)
            nc.scalar.copy(u_sb[:], ps_b[:, 0:Q * 2 * NH].rearrange("p (q n) -> p q n", q=Q)).then_inc(s_hc, 1)
            with act.Fori(0, Q) as t:
                for n in range(NH):
                    act.wait_ge(s_e, t * NH + n + 1)
                    nc.scalar.activation(p_sb[:, n], e_sb[:, n], ACT.Exp, bias=nmax[:, n:n + 1],
                                         accum_out=rsum[:, n:n + 1]).then_inc(s_p, 1)

        @block.tensor
        def _(pe):
            pe.wait_ge(s_const, 5)
            pe.wait_ge(s_x, 16)
            for q in range(Q):
                mm = nc.tensor.transpose(ps_t[0][:, q], x_sb[:, q], ident[:])
            mm.then_inc(s_tp, 1)
            pe.wait_ge(s_w, 48)
            for g in range(3):
                nc.tensor.transpose(ps_t[1][:, g], wih_sb[:, g], ident[:])
            nc.tensor.transpose(ps_t[1][:, 3], wg_sb[:].rearrange("p n d -> p (n d)"), ident[:]).then_inc(s_tp, 1)
            pe.wait_ge(s_tc, 1)
            for g in range(3):
                mm = nc.tensor.transpose(ps_t[0][:, g], whh_sb[:, g], ident[:])
            mm.then_inc(s_tp, 1)
            for j in range(Q):
                pe.wait_ge(s_tc, 2 + j)
                pe.wait_ge(s_adjf, 1)
                for q in range(Q):
                    src = adj_f[:, q].rearrange("p (s j) -> p j s", j=Q)[:, j]
                    mm = nc.tensor.transpose(ps_t[(3 + j) % 2][:, q], src, ident[:])
                mm.then_inc(s_tp, 1)
            pe.wait_ge(s_abd, 1)
            nc.tensor.matmul(ps_b[:, 0:2 * NH], wT[:, 3], a_bd[:].rearrange("p k n -> p (k n)"),
                             start=True, stop=True).then_inc(s_wa, 1)
            pe.wait_ge(s_biasrow, 1)
            for k in range(4):
                nc.tensor.matmul(ps_gate[k][:], ones_row[:], bias_row[:, k].rearrange("a q h -> a (q h)"),
                                 start=True, stop=False)
                g = [0, 1, None, 2][k]
                if g is not None:
                    for q in range(Q):
                        nc.tensor.matmul(ps_gate[k][:, q], xT[:, q], wT[:, 4 + g], start=False, stop=(k == 3 and q == Q - 1))
            with pe.Fori(0, NGROUP // 2) as it:
                for par in range(2):
                    pe.wait_ge(s_prod, it * 2 + par + 1)
                    pe.wait_ge(s_acol, it * 2 + par + 1)
                    pe.wait_ge(s_aggc, it * 2)
                    for b in range(G):
                        for j in range(Q):
                            col = b
                            mm = nc.tensor.matmul(ps_ab[par][:, col:col + 1], prod[:, par, b, j * H:(j + 1) * H],
                                                  acol[:, par, j, b:b + 1],
                                                  start=(j == 0), stop=(j == Q - 1))
                    mm.then_inc(s_agg, 1)
            pe.wait_ge(s_aggc, NGROUP)
            for k in range(3):
                for q in range(Q):
                    mm = nc.tensor.matmul(ps_gate[k][:, q], aggT[:, q], wT[:, k], start=False, stop=(q == Q - 1))
            mm.then_inc(s_gate, 1)
            pe.wait_ge(s_x1, 1)
            for q in range(Q):
                mm = nc.tensor.transpose(ps_t[0][:, q], x1[:, q], ident[:])
            mm.then_inc(s_h, 1)
            pe.wait_ge(s_hc, 1)
            pe.wait_ge(s_wacp, 1)
            for q in range(Q):
                nc.tensor.matmul(ps_a[:, q], x1T_il[:, q], wg_sb[:].rearrange("p n d -> p (n d)"), start=True, stop=True)
            for q in range(Q):
                mm = nc.tensor.matmul(ps_b[:, q * 2 * NH:(q + 1) * 2 * NH], x1T_il[:, q], wa[:], start=True, stop=True)
            mm.then_inc(s_h, 1)
            pe.wait_ge(s_wide, 1)
            for n in range(NH):
                mm = nc.tensor.matmul(ps_v[n][:], wa_wide[:, n], x1T_il, start=True, stop=True)
            mm.then_inc(s_v, 1)
            pe.wait_ge(s_hc, 3)
            with pe.Fori(0, Q) as t:
                for n in range(NH):
                    pe.wait_ge(s_p, t * NH + n + 1)
                    if n >= 2:
                        pe.wait_ge(s_ptc, t * NH + n - 1)
                    for j in range(Q):
                        mm = nc.tensor.transpose(ps_t[n % 2][:, j], p_sb[:, n, j * P:(j + 1) * P], ident[:])
                    mm.then_inc(s_pt, 1)
                    pe.wait_ge(s_ptc, t * NH + n + 1)
                    for j in range(Q):
                        mm = nc.tensor.matmul(ps_b[:, n * D:(n + 1) * D], pT[:, n, j], h_sb[:, j, n * D:(n + 1) * D],
                                              start=(j == 0), stop=(j == Q - 1))
                mm.then_inc(s_att, 1)

        @block.vector
        def _(dve):
            chain = [0]

            def link(ins):
                chain[0] += 1
                ins.then_inc(s_dv, 1)
                dve.wait_ge(s_dv, chain[0])

            dve.wait_ge(s_adj, 16)
            nc.vector.tensor_copy(adj_f[:], adj_i[:]).then_inc(s_adjf, 1)
            t = nc.vector.tensor_scalar(negm[:].rearrange("p q (j s) -> p q j s", j=Q),
                                        adj_i[:].rearrange("p q (s j) -> p q j s", j=Q), 0.0, NEG, ALU.is_le, ALU.mult)
            t.then_inc(s_neg, 1)
            dve.wait_ge(s_bias, 32)
            for k in range(2):
                nc.vector.tensor_tensor(bias_row[:, k], bias_in[:, 0, k:k + 1].broadcast_to([1, Q, H]),
                                        bias_in[:, 1, k:k + 1].broadcast_to([1, Q, H]), ALU.add)
            nc.vector.tensor_copy(bias_row[:, 2], bias_in[:, 0, 2:3].broadcast_to([1, Q, H]))
            nc.vector.tensor_copy(bias_row[:, 3], bias_in[:, 1, 2:3].broadcast_to([1, Q, H])).then_inc(s_biasrow, 1)
            dve.wait_ge(s_ac, 16 * NH)
            dve.wait_ge(s_const, 7)
            nc.vector.tensor_scalar(a_bd[:, 0], headmask[:], a_col[:, 0:1], None, ALU.mult)
            nc.vector.tensor_scalar(a_bd[:, 1], headmask[:], a_col[:, 1:2], None, ALU.mult).then_inc(s_abd, 1)
            dve.wait_ge(s_wacp, 1)
            nc.vector.tensor_copy(wa_wide[:], wa[:, 0:NH].unsqueeze(2).broadcast_to([P, NH, P])).then_inc(s_wide, 1)
            dve.wait_ge(s_xi, 16)
            with dve.Fori(0, NGROUP // NBUF) as it:
                for b in range(NBUF):
                    dve.wait_ge(s_T[b], it * 16 + 16)
                    if b >= 2:
                        dve.wait_ge(s_agg, it * NBUF + b - 1)
                    else:
                        dve.wait_ge(s_aggc, it * NBUF)
                    xb = x_il[:].rearrange("p q h -> p (q h)").unsqueeze(1).broadcast_to([P, G, Q * H])
                    nc.vector.tensor_tensor(prod[:, b % 2], T_buf[:, b], xb, ALU.mult).then_inc(s_prod, 1)

            dve.wait_ge(s_rz, 1)
            link(nc.vector.scalar_tensor_tensor(g_t[:], g_r[:], 1.0, ps_gate[3][:], ALU.add, ALU.mult))
            nc.vector.scalar_tensor_tensor(g_n[:], g_t[:], 0.5, ps_gate[2][:], ALU.mult, ALU.add).then_inc(s_npre, 1)
            dve.wait_ge(s_rz, 2)
            dve.wait_ge(s_nn, 1)
            link(nc.vector.tensor_tensor(g_t[:], x_sb[:], g_n[:], ALU.subtract))
            nc.vector.tensor_tensor(y[:], x_sb[:], g_n[:], ALU.add)
            link(nc.vector.scalar_tensor_tensor(g_t[:], g_z[:], 1.0, g_t[:], ALU.add, ALU.mult))
            link(nc.vector.scalar_tensor_tensor(y[:], g_t[:], 0.5, y[:], ALU.mult, ALU.add))

            def layernorm(src, dst, done, k):
                for q in range(Q):
                    t = nc.vector.bn_stats(st6[:, q], src[:, q])
                link(t)
                for q in range(Q):
                    t = nc.vector.bn_aggr(mv[:, q], st6[:, q])
                link(t)
                nc.vector.tensor_scalar(epsv[:], mv[:, :, 1], EPS, None, ALU.add).then_inc(s_var, 1)
                dve.wait_ge(s_rstd, k)
                for q in range(Q):
                    t = nc.vector.tensor_scalar(dst[:, q], src[:, q], mv[:, q, 0:1], rstd[:, q:q + 1],
                                                ALU.subtract, ALU.mult)
                t.then_inc(done, 1)

            layernorm(y, x1, s_x1, 1)

            dve.wait_ge(s_v, 1)
            dve.wait_ge(s_hc, 3)
            base = chain[0]
            with dve.Fori(0, Q) as t:
                at = [0]
                per = 5 + NH
                vlast = t * per + base

                def tlink(ins):
                    at[0] += 1
                    ins.then_inc(s_dv, 1)
                    dve.wait_ge(s_dv, vlast + at[0])

                u_t = u_sb[:, bass.ds(t, 1), NH:2 * NH].rearrange("p a n -> p (a n)")
                for n in range(NH):
                    ins = nc.vector.tensor_tensor(vm[:, n], ps_v[n][:].rearrange("p q h -> p (q h)"),
                                                  negm[:, bass.ds(t, 1)].rearrange("p a j -> p (a j)"), ALU.add)
                tlink(ins)
                tlink(nc.vector.tensor_reduce(vmax[:], vm[:], mybir.AxisListType.X, ALU.max))
                tlink(nc.vector.tensor_tensor(m1[:], vmax[:], u_t, ALU.add))
                tlink(nc.vector.scalar_tensor_tensor(nmax[:], m1[:], SLOPE, m1[:], ALU.mult, ALU.max))
                nc.vector.tensor_scalar(nmax[:], nmax[:], -1.0, None, ALU.mult)
                for n in range(NH):
                    tlink(nc.vector.tensor_scalar(vm[:, n], vm[:, n], u_sb[:, bass.ds(t, 1), NH + n:NH + n + 1].rearrange("p a n -> p (a n)"), None, ALU.add))
                    nc.vector.scalar_tensor_tensor(e_sb[:, n], vm[:, n], SLOPE, vm[:, n], ALU.mult, ALU.max).then_inc(s_e, 1)
                for n in range(NH):
                    dve.wait_ge(s_pt, t * NH + n + 1)
                    nc.vector.tensor_copy(pT[:, n], ps_t[n % 2][:]).then_inc(s_ptc, 1)
                dve.wait_ge(s_p, t * NH + NH)
                nc.vector.reciprocal(rinv[:], rsum[:]).then_inc(s_nn, 1)
                dve.wait_ge(s_nn, t + 2)
                dve.wait_ge(s_att, t + 1)
                tlink(nc.vector.tensor_tensor(hp[:, bass.ds(t, 1)].rearrange("p a (n d) -> p (a n) d", n=NH),
                                              ps_b[:, 0:H].rearrange("p (n d) -> p n d", n=NH),
                                              rinv[:].unsqueeze(2).broadcast_to([P, NH, D]), ALU.mult))
            chain[0] = base + Q * (5 + NH)
            link(nc.vector.tensor_tensor(y[:].rearrange("p n (q d) -> p n q d", q=Q), x1[:].rearrange("p n (q d) -> p n q d", q=Q),
                                         hp[:].rearrange("p q (n d) -> p n q d", n=NH), ALU.add))
            layernorm(y, out_sb, s_o, 2)


_INS = ["x", "adj", "L0_gnn_edge_table", "L0_gnn_w_ih", "L0_gnn_w_hh", "L0_gnn_b_ih", "L0_gnn_b_hh",
        "L1_gnn_W", "L1_gnn_a"]


def kernel(**inputs):
    import numpy as _np
    import concourse.bacc as _bacc
    from concourse import mybir as _mybir
    from concourse.bass_utils import run_bass_kernel_spmd as _run

    nc = _bacc.Bacc("TRN2", target_bir_lowering=False, num_devices=1)
    arrays, args = {}, []
    for name in _INS:
        a = _np.ascontiguousarray(inputs[name])
        arrays[f"in_{name}"] = a
        args.append(nc.dram_tensor(f"in_{name}", a.shape, _mybir.dt.from_np(a.dtype), kind="ExternalInput").ap())
    out = nc.dram_tensor("out_0", inputs["x"].shape, F32, kind="ExternalOutput").ap()
    build_gnn(nc, *args, out)
    r = _run(nc, [arrays], core_ids=[0])
    return r.results[0]["out_0"]
```

```python
from contextlib import ExitStack

import concourse.bass as bass
from concourse import mybir

F32 = mybir.dt.float32
F16 = mybir.dt.float16
BF16 = mybir.dt.bfloat16
U32 = mybir.dt.uint32
I32 = mybir.dt.int32
ALU = mybir.AluOpType
ACT = mybir.ActivationFunctionType

P = 128
EPS = 1e-5
SLOPE = 0.2
NEG = -1e30
POS_MAX = 2040.0
AX = mybir.AxisListType.X


def build_gnn(nc, x, adj, edge_table, w_ih, w_hh, b_ih, b_hh, w_gat, a_gat, out):
    N, H = x.shape
    Q = N // P
    NH, _, D = w_gat.shape
    G = 4
    NBUF = 2
    NC = 9
    B = 3
    NB = NC // B
    S = NC * P
    BS = B * P
    NGROUP = N // G
    assert H == P and NH * D == H and Q == 4

    with ExitStack() as ctx:
        def sb(name, shape, dt=F32):
            return ctx.enter_context(nc.sbuf_tensor(name, shape, dt))

        def ps(name, shape, dt=F32):
            return ctx.enter_context(nc.psum_tensor(name, shape, dt))

        def sem(name):
            return ctx.enter_context(nc.semaphore(name))

        x_sb = sb("x_sb", [P, Q, H])
        x_il = sb("x_il", [P, Q, H])
        adj_i = sb("adj_i", [P, Q, N], I32)
        wih_sb = sb("wih_sb", [P, 3, H])
        whh_sb = sb("whh_sb", [P, 3, H])
        bias_in = sb("bias_in", [1, 2, 3, H])
        wg_sb = sb("wg_sb", [P, NH, D])
        a_col = sb("a_col", [P, 2])
        ident = sb("ident", [P, P])
        ones_row = sb("ones_row", [1, P])
        bias_row = sb("bias_row", [1, 4, Q, H])
        headmask = sb("headmask", [P, NH])
        colhot32 = sb("colhot32", [P, Q, S])
        dense_area = colhot32[:].rearrange("p q s -> p (q s)")
        adj_f = dense_area[:, 0:Q * N].rearrange("p (q j) -> p q j", q=Q)
        negm = dense_area[:, Q * N:2 * Q * N].rearrange("p (q j) -> p q j", q=Q)
        adjT = sb("adjT", [P, Q, N])
        xT = sb("xT", [P, Q, P])
        wT = sb("wT", [P, 7, P])
        a_bd = sb("a_bd", [P, 2, NH])
        wa = sb("wa", [P, 2 * NH])
        wa_wide = sb("wa_wide", [P, NH, P])
        T_buf = sb("T_buf", [P, NBUF, G, Q * H])
        sparse_area = T_buf[:].rearrange("p b g f -> p (b g f)")
        vals = sparse_area[:, 0:NC * (H + NH)].rearrange("p (c f) -> p c f", c=NC)
        zmax_f = sparse_area[0:NH, NC * (H + NH):NC * (H + NH) + S]
        zmax = sparse_area[0:NH, NC * (H + NH) + S:NC * (H + NH) + 2 * S]
        prod = sb("prod", [P, 2, G, Q * H])
        acol = sb("acol", [P, 2, Q, Q])
        aggT = sb("aggT", [P, Q, P])
        iota_s = sb("iota_s", [P, S], F16)
        node_id = sb("node_id", [P, Q])
        slot_half = sb("slot_half", [P, NC])
        upper16 = sb("upper16", [P, P], F16)
        ones16 = sb("ones16", [P, P], F16)
        ident16 = sb("ident16", [P, P], F16)
        mean_col = sb("mean_col", [P, 1])
        ones_f = sb("ones_f", [P, P])
        x3 = sb("x3", [P, 3, Q, H], BF16)
        y = sb("y", [P, Q, H])
        xres = y
        ones_adj = sb("ones_adj", [P, N], F16)
        prefix = sb("prefix", [P, Q, N], F16)
        deg_pad = sb("deg_pad", [P, 2 * Q], F16)
        deg16 = deg_pad[:, Q:2 * Q]
        sums = sb("sums", [P, 2])
        totals = sb("totals", [P, 2])
        same = sb("same", [P, 1])
        flag = sb("flag", [P, 1], I32)
        base = sb("base", [P, Q])
        cum = sb("cum", [P, Q])
        pos = sb("pos", [P, Q, N], F16)
        is_ge = sb("is_ge", [P, Q, BS], F16)
        is_lt = sb("is_lt", [P, Q, BS], F16)
        rowhot = sb("rowhot", [P, Q, S], F16)
        colhot = sb("colhot", [P, Q, S], F16)
        rowhotT = sb("rowhotT", [P, NC, N])
        sgn = sb("sgn", [P, 2, N], F16)
        cnt = sb("cnt", [P, NC])
        row1 = sb("row1", [P, NC])
        row0 = sb("row0", [P, NC])
        slot_id = sb("slot_id", [P, NC])
        rowoff = sb("rowoff", [P, NC])
        eidx_f = sb("eidx_f", [P, NC])
        eidx = sb("eidx", [P, NC], U32)
        jcast = sb("jcast", [P, NC, P], F16)
        rcast = sb("rcast", [P, NC, NH], F16)
        jrow = sb("jrow", [P, S], F16)
        rrow = sb("rrow", [NH, S + 2])
        newrow = sb("newrow", [NH, S + 1])
        edge = sb("edge", [P, NC, H])
        xg = sb("xg", [P, NC, H])
        eprod = sb("eprod", [P, NC, H])
        hn_sb = sb("hn_sb", [P, Q, H])
        empty = sb("empty", [P, Q])
        erow = sb("erow", [1, Q, P])
        meanrow = sb("meanrow", [1, H + NH])
        uvres = sb("uvres", [P, Q, 2 * NH])
        uv3 = sb("uv3", [P, Q, 2 * NH, 3], BF16)
        z_sb = sb("z_sb", [P, NC, NH])
        z2 = sb("z2", [P, NC, NH])
        p_edge = sb("p_edge", [P, NC, NH])
        dinv = sb("dinv", [P, Q, NH])
        g_r = sb("g_r", [P, Q, H])
        g_z = sb("g_z", [P, Q, H])
        g_n = sb("g_n", [P, Q, H])
        g_t = sb("g_t", [P, Q, H])
        st6 = sb("st6", [P, Q, 6])
        mv = sb("mv", [P, Q, 2])
        epsv = sb("epsv", [P, Q])
        mhalf = sb("mhalf", [P, Q])
        rstd = sb("rstd", [P, Q])
        x1 = sb("x1", [P, Q, H])
        x1T = sb("x1T", [P, Q, P])
        x1T_il = x1T[:].rearrange("h t p -> h (t p)").rearrange("h (s q) -> h q s", q=Q)
        h_sb = sb("h_sb", [P, Q, H])
        u_sb = sb("u_sb", [P, Q, 2 * NH])
        vm = T_buf[:].rearrange("p b g f -> p (b g f)")[:, 0:NH * N].rearrange("p (n j) -> p n j", n=NH)
        vmax = sb("vmax", [P, NH])
        m1 = sb("m1", [P, NH])
        nmax = sb("nmax", [P, NH])
        e_sb = T_buf[:].rearrange("p b g f -> p (b g f)")[:, NH * N:2 * NH * N].rearrange("p (n j) -> p n j", n=NH)
        p_sb = prod[:].rearrange("p b g f -> p (b g f)")[:, 0:NH * N].rearrange("p (n j) -> p n j", n=NH)
        rsum = sb("rsum", [P, NH])
        rinv = sb("rinv", [P, NH])
        pT = prod[:].rearrange("p b g f -> p (b g f)")[:, NH * N:2 * NH * N].rearrange("p (n q i) -> p n q i", n=NH, q=Q)
        hp = sb("hp", [P, Q, H])
        out_sb = g_n

        ps_gate = [ps(f"ps_gate{k}", [P, Q, H]) for k in range(4)]
        ps_v = ps_gate
        ps_t = [ps(f"ps_t{k}", [P, 4, P]) for k in range(2)]
        ps_a = ps("ps_a", [P, Q, P])
        ps_b = ps("ps_b", [P, 512])
        sel_bank = [ps_t[k][:].rearrange("p q i -> p (q i)") for k in range(2)]
        xg_bank = [ps_a[:].rearrange("p q i -> p (q i)"), ps_gate[3][:].rearrange("p q h -> p (q h)")]
        agg_bank = ps_b[:]
        z_bank = ps_gate[0][:].rearrange("p q h -> p (q h)")
        zT_bank = [ps_t[0][:].rearrange("p q i -> p (q i)"), ps_t[1][:].rearrange("p q i -> p (q i)"),
                   ps_gate[1][:].rearrange("p q h -> p (q h)")]
        hg_bank = [ps_gate[2][:].rearrange("p q h -> p (q h)"), ps_gate[3][:].rearrange("p q h -> p (q h)"), ps_b[:]]
        num_bank = [ps_t[k][:].rearrange("p q i -> p (q i)")[:, 0:2 * (H + NH)].rearrange("p (q f) -> p q f", q=2)
                    for k in range(2)]
        row_bank = ps_gate[2][:].rearrange("p q h -> p (q h)")
        ps_ab = [ps_a[:].rearrange("p q i -> p (q i)"), ps_b[:]]

        s_x = sem("s_x"); s_xi = sem("s_xi"); s_adj = [sem(f"s_adj{q}") for q in range(Q)]; s_w = sem("s_w"); s_bias = sem("s_bias"); s_ac = sem("s_ac")
        s_T = [sem(f"s_T{b}") for b in range(NBUF)]
        s_const = sem("s_const"); s_biasrow = sem("s_biasrow"); s_abd = sem("s_abd")
        s_wide = sem("s_wide"); s_wa = sem("s_wa"); s_wacp = sem("s_wacp")
        s_adjf = sem("s_adjf"); s_neg = sem("s_neg")
        s_tp = sem("s_tp"); s_tc = sem("s_tc")
        s_prod = sem("s_prod"); s_acol = sem("s_acol"); s_agg = sem("s_agg"); s_aggc = sem("s_aggc")
        s_gate = sem("s_gate"); s_rz = sem("s_rz"); s_dv = sem("s_dv"); s_nn = sem("s_nn"); s_npre = sem("s_npre")
        s_var = sem("s_var"); s_rstd = sem("s_rstd"); s_x1 = sem("s_x1")
        s_h = sem("s_h"); s_hc = sem("s_hc"); s_v = sem("s_v")
        s_e = sem("s_e"); s_p = sem("s_p"); s_pt = sem("s_pt"); s_ptc = sem("s_ptc"); s_att = sem("s_att")
        s_slot = sem("s_slot"); s_hnc = sem("s_hnc"); s_basec = sem("s_basec"); s_adjTp = sem("s_adjTp"); s_adjT = sem("s_adjT"); s_x1T = sem("s_x1T"); s_uc = sem("s_uc"); s_ri = sem("s_ri"); s_iota = sem("s_iota"); s_c16 = sem("s_c16"); s_x3 = sem("s_x3"); s_scan = sem("s_scan"); s_sq = sem("s_sq")
        s_sum = sem("s_sum"); s_base = sem("s_base"); s_tot = sem("s_tot"); s_flag = sem("s_flag"); s_pos = sem("s_pos")
        s_hn = sem("s_hn"); s_row = sem("s_row"); s_sel = sem("s_sel"); s_cnt = sem("s_cnt"); s_idx = sem("s_idx")
        s_cast = sem("s_cast"); s_jr = sem("s_jr"); s_jrc = sem("s_jrc"); s_col = sem("s_col"); s_c32 = sem("s_c32")
        s_rr = sem("s_rr"); s_rrc = sem("s_rrc"); s_xg = sem("s_xg"); s_xgc = sem("s_xgc")
        s_edge = [sem(f"s_edge{c}") for c in range(NC)]
        s_ep = sem("s_ep"); s_rT = sem("s_rT"); s_aggs = sem("s_aggs"); s_aggT = sem("s_aggT")
        s_emp = sem("s_emp"); s_er = sem("s_er"); s_erc = sem("s_erc"); s_new = sem("s_new")
        s_uv3 = sem("s_uv3"); s_z = sem("s_z"); s_zs = sem("s_zs"); s_zT = sem("s_zT"); s_zm = sem("s_zm"); s_mT = sem("s_mT")
        s_hg = sem("s_hg"); s_mean = sem("s_mean"); s_meanc = sem("s_meanc"); s_ze = sem("s_ze"); s_pe = sem("s_pe")
        s_vals = sem("s_vals"); s_num = sem("s_num"); s_ds = sem("s_ds"); s_dd = sem("s_dd"); s_pl = sem("s_pl")
        s_o = sem("s_o"); s_out = sem("s_out")

        x_v = x.rearrange("(p q) h -> p q h", q=Q)
        out_v = out.rearrange("(t p) h -> p t h", p=P)
        adj_v = adj.rearrange("(p q) j -> p q j", q=Q)
        T_v = edge_table.rearrange("(i p q) h -> i p (q h)", p=P, q=Q)

        block = ctx.enter_context(nc.Block())

        def batch(b):
            return slice(b * BS, (b + 1) * BS)

        @block.sync
        def _(sp):
            for q in range(Q):
                sp.dma_start(adj_i[:, q], adj_v[:, q]).then_inc(s_adj[q], 16)
            sp.dma_start(wih_sb[:], w_ih.rearrange("(g p) h -> p g h", p=P)).then_inc(s_w, 16)
            sp.dma_start(whh_sb[:], w_hh.rearrange("(g p) h -> p g h", p=P)).then_inc(s_w, 16)
            sp.wait_ge(s_flag, 1)
            sparse = sp.value_load(flag[0:1, 0:1], min_val=0, max_val=1)
            with sp.If(sparse == 0):
                for b in range(NBUF):
                    sp.dma_start(T_buf[:, b], T_v[b * G:(b + 1) * G].rearrange("i p f -> p i f")).then_inc(s_T[b], 16)
                with sp.Fori(0, NGROUP // NBUF - 1) as it:
                    for b in range(NBUF):
                        sp.wait_ge(s_prod, it * NBUF + b + 1)
                        src = T_v[bass.ds((it * NBUF + b + NBUF) * G, G)].rearrange("i p f -> p i f")
                        sp.dma_start(T_buf[:, b], src).then_inc(s_T[b], 16)
            sp.wait_ge(s_o, 1)
            sp.dma_start(out_v, out_sb[:]).then_inc(s_out, 16)
            sp.wait_ge(s_out, 16)

        @block.gpsimd
        def _(pool):
            nc.gpsimd.memset(ident[:], 0.0).then_inc(s_const, 1)
            nc.gpsimd.memset(headmask[:], 1.0).then_inc(s_const, 1)
            nc.gpsimd.memset(upper16[:], 0.0).then_inc(s_const, 1)
            nc.gpsimd.iota(iota_s[:], [[1, S]], base=0, channel_multiplier=0,
                           allow_small_or_imprecise_dtypes=True).then_inc(s_iota, 1)
            nc.gpsimd.iota(node_id[:], [[1, Q]], base=0, channel_multiplier=Q,
                           allow_small_or_imprecise_dtypes=True).then_inc(s_iota, 1)
            nc.gpsimd.iota(slot_id[:], [[P, NC]], base=0, channel_multiplier=1,
                           allow_small_or_imprecise_dtypes=True).then_inc(s_iota, 1)
            pool.wait_ge(s_const, 3)
            nc.gpsimd.affine_select(out=ident[:], in_=ident[:], compare_op=ALU.not_equal, fill=1.0, base=0,
                                    pattern=[[-1, P]], channel_multiplier=1).then_inc(s_const, 1)
            nc.gpsimd.affine_select(out=headmask[:], in_=headmask[:], compare_op=ALU.is_ge, fill=0.0, base=0,
                                    pattern=[[-D, NH]], channel_multiplier=1).then_inc(s_const, 1)
            nc.gpsimd.affine_select(out=upper16[:], in_=upper16[:], compare_op=ALU.is_ge, fill=1.0, base=0,
                                    pattern=[[-1, P]], channel_multiplier=1).then_inc(s_const, 1)
            pool.wait_ge(s_const, 6)
            nc.gpsimd.affine_select(out=headmask[:], in_=headmask[:], compare_op=ALU.is_ge, fill=0.0, base=D - 1,
                                    pattern=[[D, NH]], channel_multiplier=-1).then_inc(s_const, 1)
            pool.wait_ge(s_xi, 16)
            nc.gpsimd.tensor_copy(x3[:, 0], x_il[:]).then_inc(s_x3, 1)
            pool.wait_ge(s_x3, 1)
            nc.gpsimd.tensor_tensor(xres[:], x_il[:], x3[:, 0], ALU.subtract).then_inc(s_x3, 1)
            pool.wait_ge(s_x3, 2)
            nc.gpsimd.tensor_copy(x3[:, 1], xres[:]).then_inc(s_x3, 1)
            pool.wait_ge(s_x3, 3)
            nc.gpsimd.tensor_tensor(x3[:, 2], xres[:], x3[:, 1], ALU.subtract).then_inc(s_x3, 1)
            for b in range(NB):
                pool.wait_ge(s_idx, b + 1)
                for c in range(b * B, (b + 1) * B):
                    nc.gpsimd.indirect_dma_start(
                        out=edge[:, c], out_offset=None, in_=edge_table,
                        in_offset=bass.IndirectOffsetOnAxis(ap=eidx[:, c:c + 1], axis=0)).then_inc(s_edge[c], 16)
            pool.wait_ge(s_col, NB)
            for q in range(Q):
                t = nc.gpsimd.tensor_copy(colhot32[:, q], colhot[:, q])
            t.then_inc(s_c32, 1)
            pool.wait_ge(s_flag, 1)
            sparse = pool.value_load(flag[0:1, 0:1], min_val=0, max_val=1)
            with pool.If(sparse == 0):
                pool.wait_ge(s_adjT, Q)
                with pool.Fori(0, NGROUP // 2) as it:
                    for par in range(2):
                        pool.wait_ge(s_agg, it * 2)
                        src = adjT[:].rearrange("p j (q i) -> p j q i", q=Q)[:, :, :, bass.ds(it * 2 + par, 1)]
                        nc.gpsimd.tensor_copy(acol[:, par].unsqueeze(3), src).then_inc(s_acol, 1)
            for k in range(2):
                pool.wait_ge(s_var, k + 1)
                nc.gpsimd.tensor_tensor(rstd[:], epsv[:], mhalf[:], ALU.pow).then_inc(s_rstd, 1)

        @block.scalar
        def _(act):
            act.dma_start(x_sb[:], x.rearrange("(t p) h -> p t h", p=P)).then_inc(s_x, 16)
            act.dma_start(x_il[:], x_v).then_inc(s_xi, 16)
            act.dma_start(wg_sb[:], w_gat.rearrange("n p d -> p n d")).then_inc(s_w, 16)
            act.dma_start(bias_in[:, 0], b_ih.rearrange("(a g h) -> a g h", a=1, g=3)).then_inc(s_bias, 16)
            act.dma_start(bias_in[:, 1], b_hh.rearrange("(a g h) -> a g h", a=1, g=3)).then_inc(s_bias, 16)
            with nc.allow_non_contiguous_dma(reason="256 attention weights"):
                for n in range(NH):
                    act.dma_start(a_col[n * D:(n + 1) * D, :],
                                  a_gat[n, :, 0].rearrange("(k d) -> d k", k=2)).then_inc(s_ac, 16)
            act.wait_ge(s_tp, 1)
            nc.scalar.copy(xT[:], ps_t[0][:]).then_inc(s_tc, 1)
            act.wait_ge(s_tp, 2)
            nc.scalar.copy(wT[:, 0:4], ps_t[1][:]).then_inc(s_tc, 1)
            act.wait_ge(s_tp, 3)
            nc.scalar.copy(wT[:, 4:7], ps_t[0][:, 0:3]).then_inc(s_tc, 1)
            act.wait_ge(s_wa, 1)
            nc.scalar.copy(wa[:], ps_b[:, 0:2 * NH]).then_inc(s_wacp, 1)
            for q in range(Q):
                act.wait_ge(s_adj[q], 16)
            nc.scalar.activation(rowhotT[:, 0:Q], adj_i[:], ACT.Square, accum_out=sums[:, 0:1]).then_inc(s_sq, 1)
            act.wait_ge(s_hn, 1)
            nc.scalar.copy(hn_sb[:], ps_gate[3][:]).then_inc(s_hnc, 1)
            act.wait_ge(s_slot, 1)

            def count(b):
                for c in range(b * B, (b + 1) * B):
                    act.wait_ge(s_sel, c + 1)
                    nc.scalar.activation(sgn[:, c % 2, 0:N - 1], sel_bank[c % 2][:, 0:N - 1], ACT.Sign, scale=-1.0,
                                         bias=slot_half[:, c:c + 1], accum_out=cnt[:, c:c + 1])
                    nc.scalar.copy(row1[:, c:c + 1], sel_bank[c % 2][:, N - 1:N]).then_inc(s_cnt, 1)

            def keep_jrow(b):
                act.wait_ge(s_jr, b + 1)
                nc.scalar.copy(jrow[:, batch(b)], row_bank[:, 0:BS]).then_inc(s_jrc, 1)

            def keep_xg_rrow(b):
                act.wait_ge(s_xg, b + 1)
                nc.scalar.copy(xg[:, b * B:(b + 1) * B].rearrange("p c h -> p (c h)"), xg_bank[b % 2][:, 0:BS])\
                    .then_inc(s_xgc, 1)
                act.wait_ge(s_rr, b + 1)
                nc.scalar.copy(rrow[:, 1 + b * BS:1 + (b + 1) * BS], row_bank[0:NH, 0:BS]).then_inc(s_rrc, 1)

            count(0)
            count(1)
            keep_jrow(0)
            count(2)
            keep_xg_rrow(0)
            keep_jrow(1)
            keep_xg_rrow(1)
            keep_jrow(2)
            keep_xg_rrow(2)
            act.wait_ge(s_er, 1)
            nc.scalar.copy(erow[:].rearrange("a q p -> a (q p)"), row_bank[0:1, :]).then_inc(s_erc, 1)
            act.wait_ge(s_aggs, 1)
            nc.scalar.copy(aggT[:].rearrange("h t p -> h (t p)"), agg_bank).then_inc(s_aggT, 1)
            sparse = act.value_load(flag[0:1, 0:1], min_val=0, max_val=1)
            with act.If(sparse == 0):
                for j in range(Q):
                    act.wait_ge(s_adjTp, j + 1)
                    nc.scalar.copy(adjT[:, j], ps_t[j % 2][:].rearrange("p q i -> p (q i)")).then_inc(s_adjT, 1)
                with act.Fori(0, NGROUP // 2) as it:
                    for par in range(2):
                        act.wait_ge(s_agg, it * 2 + par + 1)
                        dst = aggT[:].rearrange("h t p -> h (t p)")[:, bass.ds((it * 2 + par) * G, G)]
                        nc.scalar.copy(dst, ps_ab[par][:, 0:G]).then_inc(s_aggc, 1)
            act.wait_ge(s_gate, 1)
            nc.scalar.activation(g_r[:], ps_gate[0][:], ACT.Tanh, scale=0.5).then_inc(s_rz, 1)
            nc.scalar.activation(g_z[:], ps_gate[1][:], ACT.Tanh, scale=0.5).then_inc(s_rz, 1)
            act.wait_ge(s_npre, 1)
            nc.scalar.activation(g_n[:], g_n[:], ACT.Tanh).then_inc(s_nn, 1)
            act.wait_ge(s_h, 1)
            nc.scalar.copy(x1T[:], ps_t[0][:]).then_inc(s_x1T, 1)
            act.wait_ge(s_h, 3)
            nc.scalar.copy(h_sb[:], ps_a[:]).then_inc(s_hc, 1)
            with act.If(sparse == 0):
                with act.Fori(0, Q) as t:
                    for n in range(NH):
                        act.wait_ge(s_e, t * NH + n + 1)
                        nc.scalar.activation(p_sb[:, n], e_sb[:, n], ACT.Exp, bias=nmax[:, n:n + 1],
                                             accum_out=rsum[:, n:n + 1]).then_inc(s_p, 1)
            with act.Else():
                act.wait_ge(s_mean, 1)
                nc.scalar.copy(meanrow[:, 0:H], ps_a[0:1, 0].rearrange("a i -> a i")).then_inc(s_meanc, 1)
                act.wait_ge(s_ze, 1)
                nc.scalar.activation(p_edge[:], z_sb[:], ACT.Exp).then_inc(s_pe, 1)

        @block.tensor
        def _(pe):
            pe.wait_ge(s_const, 4)
            pe.wait_ge(s_x, 16)
            for q in range(Q):
                mm = nc.tensor.transpose(ps_t[0][:, q], x_sb[:, q], ident[:])
            mm.then_inc(s_tp, 1)
            pe.wait_ge(s_w, 48)
            for g in range(3):
                nc.tensor.transpose(ps_t[1][:, g], wih_sb[:, g], ident[:])
            nc.tensor.transpose(ps_t[1][:, 3], wg_sb[:].rearrange("p n d -> p (n d)"), ident[:]).then_inc(s_tp, 1)
            pe.wait_ge(s_tc, 1)
            for g in range(3):
                mm = nc.tensor.transpose(ps_t[0][:, g], whh_sb[:, g], ident[:])
            mm.then_inc(s_tp, 1)
            pe.wait_ge(s_tc, 3)
            pe.wait_ge(s_abd, 1)
            nc.tensor.matmul(ps_b[:, 0:2 * NH], wT[:, 3], a_bd[:].rearrange("p k n -> p (k n)"),
                             start=True, stop=True).then_inc(s_wa, 1)

            def bias(k):
                nc.tensor.matmul(ps_gate[k][:], ones_row[:], bias_row[:, k].rearrange("a q h -> a (q h)"),
                                 start=True, stop=False)

            pe.wait_ge(s_biasrow, 1)
            for k, g in ((3, 2), (0, 0), (1, 1)):
                bias(k)
                for q in range(Q):
                    mm = nc.tensor.matmul(ps_gate[k][:, q], xT[:, q], wT[:, 4 + g], start=False,
                                          stop=(k == 3 and q == Q - 1))
                if k == 3:
                    mm.then_inc(s_hn, 1)
            pe.wait_ge(s_wacp, 1)
            pe.wait_ge(s_sum, 1)
            for n in range(Q):
                mm = nc.tensor.matmul(ps_b[:, 0:Q], upper16[:] if n == 0 else ones16[:], deg_pad[:, Q - n:2 * Q - n],
                                      start=(n == 0), stop=(n == Q - 1))
            mm.then_inc(s_base, 1)
            pe.wait_ge(s_sq, 1)
            pe.wait_ge(s_basec, 1)
            nc.tensor.matmul(ps_b[:, 0:2], ones_f[:], sums[:], start=True, stop=True).then_inc(s_tot, 1)

            def select(b):
                pe.wait_ge(s_row, b + 1)
                pe.wait_ge(s_pos, 1)
                for c in range(b * B, (b + 1) * B):
                    if c >= 2:
                        pe.wait_ge(s_cnt, c - 1)
                    for q in range(Q):
                        mm = nc.tensor.matmul(sel_bank[c % 2], rowhot[:, q, c * P:(c + 1) * P], pos[:, q],
                                              start=(q == 0), stop=(q == Q - 1))
                    mm.then_inc(s_sel, 1)

            def source_row(b):
                pe.wait_ge(s_cast, b + 1)
                if b >= 1:
                    pe.wait_ge(s_rrc, b)
                for c in range(b * B, (b + 1) * B):
                    mm = nc.tensor.matmul(row_bank[:, (c - b * B) * P:(c - b * B + 1) * P], jcast[:, c], ident16[:],
                                          start=True, stop=True)
                mm.then_inc(s_jr, 1)

            def target_row(b):
                pe.wait_ge(s_jrc, b + 1)
                for c in range(b * B, (b + 1) * B):
                    mm = nc.tensor.matmul(row_bank[0:NH, (c - b * B) * P:(c - b * B + 1) * P], rcast[:, c], ident16[:],
                                          start=True, stop=True)
                mm.then_inc(s_rr, 1)

            def source_features(b):
                pe.wait_ge(s_col, b + 1)
                if b == 0:
                    pe.wait_ge(s_x3, 4)
                    pe.wait_ge(s_hnc, 1)
                if b >= 2:
                    pe.wait_ge(s_xgc, b - 1)
                for c in range(b * B, (b + 1) * B):
                    for q in range(Q):
                        for k in range(3):
                            mm = nc.tensor.matmul(xg_bank[b % 2][:, (c - b * B) * P:(c - b * B + 1) * P],
                                                  colhot[:, q, c * P:(c + 1) * P], x3[:, k, q],
                                                  start=(q == 0 and k == 0), stop=(q == Q - 1 and k == 2))
                mm.then_inc(s_xg, 1)

            def aggregate(b):
                for c in range(b * B, (b + 1) * B):
                    pe.wait_ge(s_rT, c + 1)
                    pe.wait_ge(s_ep, c + 1)
                    mm = nc.tensor.matmul(agg_bank, eprod[:, c], rowhotT[:, c], start=(c == 0), stop=(c == NC - 1))
                if b == NB - 1:
                    mm.then_inc(s_aggs, 1)

            select(0)
            select(1)
            source_row(0)
            select(2)
            source_features(0)
            target_row(0)
            source_row(1)
            pe.wait_ge(s_flag, 1)
            aggregate(0)
            source_features(1)
            target_row(1)
            source_row(2)
            aggregate(1)
            source_features(2)
            target_row(2)
            pe.wait_ge(s_rrc, NB)
            pe.wait_ge(s_emp, 1)
            for q in range(Q):
                mm = nc.tensor.transpose(row_bank[0:1, q * P:(q + 1) * P], empty[:, q:q + 1], ident[:])
            mm.then_inc(s_er, 1)
            aggregate(2)
            pe.wait_ge(s_erc, 1)
            bias(2)
            sparse = pe.value_load(flag[0:1, 0:1], min_val=0, max_val=1)
            with pe.If(sparse == 0):
                pe.wait_ge(s_adjf, 1)
                pe.wait_ge(s_aggT, 1)
                for j in range(Q):
                    if j >= 2:
                        pe.wait_ge(s_adjT, j - 1)
                    for q in range(Q):
                        src = adj_f[:, q].rearrange("p (s j) -> p j s", j=Q)[:, j]
                        mm = nc.tensor.transpose(ps_t[j % 2][:, q], src, ident[:])
                    mm.then_inc(s_adjTp, 1)
                with pe.Fori(0, NGROUP // 2) as it:
                    for par in range(2):
                        pe.wait_ge(s_prod, it * 2 + par + 1)
                        pe.wait_ge(s_acol, it * 2 + par + 1)
                        pe.wait_ge(s_aggc, it * 2)
                        for b in range(G):
                            for j in range(Q):
                                mm = nc.tensor.matmul(ps_ab[par][:, b:b + 1], prod[:, par, b, j * H:(j + 1) * H],
                                                      acol[:, par, j, b:b + 1], start=(j == 0), stop=(j == Q - 1))
                        mm.then_inc(s_agg, 1)
                pe.wait_ge(s_aggc, NGROUP)
            pe.wait_ge(s_aggT, 1)
            for k in range(3):
                for q in range(Q):
                    mm = nc.tensor.matmul(ps_gate[k][:, q], aggT[:, q], wT[:, k], start=False, stop=(q == Q - 1))
            mm.then_inc(s_gate, 1)
            pe.wait_ge(s_x1, 1)
            for q in range(Q):
                mm = nc.tensor.transpose(ps_t[0][:, q], x1[:, q], ident[:])
            mm.then_inc(s_h, 1)
            pe.wait_ge(s_x1T, 1)
            for q in range(Q):
                mm = nc.tensor.matmul(ps_b[:, q * 2 * NH:(q + 1) * 2 * NH], x1T_il[:, q], wa[:], start=True, stop=True)
            mm.then_inc(s_h, 1)
            for q in range(Q):
                mm = nc.tensor.matmul(ps_a[:, q], x1T_il[:, q], wg_sb[:].rearrange("p n d -> p (n d)"),
                                      start=True, stop=True)
            mm.then_inc(s_h, 1)
            with pe.If(sparse == 0):
                pe.wait_ge(s_wide, 1)
                for n in range(NH):
                    mm = nc.tensor.matmul(ps_v[n][:], wa_wide[:, n], x1T_il, start=True, stop=True)
                mm.then_inc(s_v, 1)
                pe.wait_ge(s_hc, 1)
                pe.wait_ge(s_uc, 1)
                with pe.Fori(0, Q) as t:
                    for n in range(NH):
                        pe.wait_ge(s_p, t * NH + n + 1)
                        if n >= 2:
                            pe.wait_ge(s_ptc, t * NH + n - 1)
                        for j in range(Q):
                            mm = nc.tensor.transpose(ps_t[n % 2][:, j], p_sb[:, n, j * P:(j + 1) * P], ident[:])
                        mm.then_inc(s_pt, 1)
                        pe.wait_ge(s_ptc, t * NH + n + 1)
                        for j in range(Q):
                            mm = nc.tensor.matmul(ps_b[:, n * D:(n + 1) * D], pT[:, n, j], h_sb[:, j, n * D:(n + 1) * D],
                                                  start=(j == 0), stop=(j == Q - 1))
                    mm.then_inc(s_att, 1)
            with pe.Else():
                pe.wait_ge(s_uv3, 1)
                for b in range(NB):
                    for c in range(b * B, (b + 1) * B):
                        at = z_bank[:, c * 3 * NH:(c + 1) * 3 * NH]
                        for q in range(Q):
                            nc.tensor.matmul(at, rowhot[:, q, c * P:(c + 1) * P],
                                             uv3[:, q, NH:2 * NH].rearrange("p n k -> p (n k)"),
                                             start=(q == 0), stop=False)
                        for q in range(Q):
                            mm = nc.tensor.matmul(at, colhot[:, q, c * P:(c + 1) * P],
                                                  uv3[:, q, 0:NH].rearrange("p n k -> p (n k)"),
                                                  start=False, stop=(q == Q - 1))
                mm.then_inc(s_z, 1)
                pe.wait_ge(s_hc, 1)
                for q in range(Q):
                    mm = nc.tensor.matmul(ps_a[0:1, 0], mean_col[:], h_sb[:, q], start=(q == 0), stop=(q == Q - 1))
                mm.then_inc(s_mean, 1)
                pe.wait_ge(s_zs, 1)
                for b in range(NB):
                    for c in range(b * B, (b + 1) * B):
                        mm = nc.tensor.transpose(zT_bank[b][0:NH, (c - b * B) * P:(c - b * B + 1) * P], z2[:, c], ident[:])
                    mm.then_inc(s_zT, 1)

                def gather_h(b):
                    for c in range(b * B, (b + 1) * B):
                        for q in range(Q):
                            mm = nc.tensor.matmul(hg_bank[b][:, (c - b * B) * P:(c - b * B + 1) * P],
                                                  colhot32[:, q, c * P:(c + 1) * P], h_sb[:, q],
                                                  start=(q == 0), stop=(q == Q - 1))
                    mm.then_inc(s_hg, 1)

                pe.wait_ge(s_c32, 1)
                pe.wait_ge(s_uc, 1)
                gather_h(0)
                gather_h(1)
                pe.wait_ge(s_zm, 1)
                for c in range(NC):
                    mm = nc.tensor.transpose(z_bank[:, c * NH:(c + 1) * NH], zmax[:, c * P:(c + 1) * P], ident[0:NH, 0:NH])
                mm.then_inc(s_mT, 1)
                gather_h(2)
                pe.wait_ge(s_meanc, 1)
                for c in range(NC):
                    pe.wait_ge(s_vals, c // B + 1)
                    for q in range(Q):
                        nc.tensor.matmul(num_bank[q // 2][:, q % 2], rowhotT[:, c].rearrange("s (p q) -> s q p", q=Q)[:, q],
                                         vals[:, c], start=(c == 0 and q % 2 == 0), stop=False, skip_group_check=True)
                for q in range(Q):
                    mm = nc.tensor.matmul(num_bank[q // 2][:, q % 2], erow[:, q], meanrow[:], start=False, stop=True,
                                          skip_group_check=True)
                mm.then_inc(s_num, 1)

        @block.vector
        def _(dve):
            chain = [0]

            def link(ins):
                chain[0] += 1
                ins.then_inc(s_dv, 1)
                dve.wait_ge(s_dv, chain[0])

            nc.vector.memset(ones_adj[:], 1.0).then_inc(s_c16, 1)
            nc.vector.memset(ones16[:], 1.0).then_inc(s_c16, 1)
            nc.vector.memset(ones_f[:], 1.0).then_inc(s_c16, 1)
            nc.vector.memset(ones_row[:], 1.0)
            nc.vector.memset(deg_pad[:, 0:Q], 0.0)
            nc.vector.memset(mean_col[:], 1.0 / N)
            nc.vector.memset(mhalf[:], -0.5)
            nc.vector.memset(meanrow[:, H:H + NH], 1.0)
            nc.vector.memset(rrow[:, 0:1], -1.0)
            nc.vector.memset(rrow[:, S + 1:S + 2], -1.0)
            dve.wait_ge(s_bias, 32)
            for k in range(2):
                nc.vector.tensor_tensor(bias_row[:, k], bias_in[:, 0, k:k + 1].broadcast_to([1, Q, H]),
                                        bias_in[:, 1, k:k + 1].broadcast_to([1, Q, H]), ALU.add)
            nc.vector.tensor_copy(bias_row[:, 2], bias_in[:, 0, 2:3].broadcast_to([1, Q, H]))
            nc.vector.tensor_copy(bias_row[:, 3], bias_in[:, 1, 2:3].broadcast_to([1, Q, H])).then_inc(s_biasrow, 1)
            dve.wait_ge(s_const, 7)
            nc.vector.tensor_copy(ident16[:], ident[:])
            dve.wait_ge(s_iota, 3)
            nc.vector.tensor_scalar(slot_half[:], slot_id[:], 0.5, None, ALU.add).then_inc(s_slot, 1)
            dve.wait_ge(s_ac, 16 * NH)
            nc.vector.tensor_scalar(a_bd[:, 0], headmask[:], a_col[:, 0:1], None, ALU.mult)
            nc.vector.tensor_scalar(a_bd[:, 1], headmask[:], a_col[:, 1:2], None, ALU.mult).then_inc(s_abd, 1)

            dve.wait_ge(s_c16, 1)
            for q in range(Q):
                dve.wait_ge(s_adj[q], 16)
                t = nc.vector.tensor_tensor_scan(prefix[:, q], ones_adj[:], adj_i[:, q], 0.0, ALU.mult, ALU.add)
            link(t)
            link(nc.vector.tensor_copy(deg16, prefix[:, :, N - 1]))
            nc.vector.tensor_reduce(sums[:, 1:2], deg16, AX, ALU.add).then_inc(s_sum, 1)
            nc.vector.tensor_scalar(empty[:], deg16, 0.0, None, ALU.is_equal).then_inc(s_emp, 1)
            dve.wait_ge(s_base, 1)
            nc.vector.tensor_tensor(cum[:], ps_b[:, 0:Q], deg16, ALU.add)
            nc.vector.tensor_copy(base[:], ps_b[:, 0:Q]).then_inc(s_basec, 1)
            dve.wait_ge(s_basec, 1)

            def row_onehot(b):
                for q in range(Q):
                    nc.vector.tensor_scalar(is_ge[:, q], iota_s[:, batch(b)], base[:, q:q + 1], None, ALU.is_ge)
                    t = nc.vector.tensor_scalar(is_lt[:, q], iota_s[:, batch(b)], cum[:, q:q + 1], None, ALU.is_lt)
                link(t)
                nc.vector.tensor_tensor(rowhot[:, :, batch(b)], is_ge[:], is_lt[:], ALU.mult).then_inc(s_row, 1)

            row_onehot(0)
            for q in range(Q):
                t = nc.vector.tensor_scalar(pos[:, q], prefix[:, q], base[:, q:q + 1], POS_MAX, ALU.add, ALU.min)
            link(t)
            nc.vector.tensor_scalar(pos[:, :, N - 1], node_id[:], 1.0, None, ALU.add).then_inc(s_pos, 1)

            def edge_index(b):
                cs = slice(b * B, (b + 1) * B)
                dve.wait_ge(s_cnt, (b + 1) * B)
                link(nc.vector.tensor_scalar(rowoff[:, cs], row1[:, cs], float(N), (N - 1) / 2 - N, ALU.mult, ALU.add))
                link(nc.vector.scalar_tensor_tensor(eidx_f[:, cs], cnt[:, cs], 0.5, rowoff[:, cs], ALU.mult, ALU.add))
                nc.vector.tensor_scalar(eidx[:, cs], eidx_f[:, cs], 0.0, float(N * N - 1), ALU.max, ALU.min)\
                    .then_inc(s_idx, 1)
                nc.vector.tensor_scalar(jcast[:, cs], cnt[:, cs].unsqueeze(2).broadcast_to([P, B, P]),
                                        0.5, (N - 1) / 2, ALU.mult, ALU.add)
                nc.vector.tensor_copy(rcast[:, cs], row1[:, cs].unsqueeze(2).broadcast_to([P, B, NH])).then_inc(s_cast, 1)
                link(nc.vector.tensor_scalar(row0[:, cs], row1[:, cs], -1.0, None, ALU.add))

            def col_onehot(b):
                dve.wait_ge(s_jrc, b + 1)
                for q in range(Q):
                    t = nc.vector.tensor_scalar(colhot[:, q, batch(b)], jrow[:, batch(b)], node_id[:, q:q + 1], None,
                                                ALU.is_equal)
                t.then_inc(s_col, 1)

            def row_onehot_T(b):
                for c in range(b * B, (b + 1) * B):
                    nc.vector.tensor_scalar(rowhotT[:, c], iota_s[:, 0:N], row0[:, c:c + 1], None, ALU.is_equal)\
                        .then_inc(s_rT, 1)

            def products(b):
                dve.wait_ge(s_xgc, b + 1)
                for c in range(b * B, (b + 1) * B):
                    dve.wait_ge(s_edge[c], 16)
                    nc.vector.tensor_tensor(eprod[:, c], edge[:, c], xg[:, c], ALU.mult).then_inc(s_ep, 1)

            row_onehot(1)
            edge_index(0)
            row_onehot(2)
            edge_index(1)
            col_onehot(0)
            dve.wait_ge(s_tot, 1)
            link(nc.vector.tensor_copy(totals[:], ps_b[:, 0:2]))
            link(nc.vector.tensor_tensor(same[:], totals[:, 0:1], totals[:, 1:2], ALU.is_equal))
            nc.vector.scalar_tensor_tensor(flag[:], totals[:, 1:2], float(S), same[:], ALU.is_le, ALU.mult)\
                .then_inc(s_flag, 1)
            edge_index(2)
            row_onehot_T(0)
            col_onehot(1)
            products(0)
            row_onehot_T(1)
            col_onehot(2)
            products(1)
            row_onehot_T(2)
            products(2)
            dve.wait_ge(s_rrc, NB)
            link(nc.vector.tensor_tensor(newrow[:], rrow[:, 1:S + 2], rrow[:, 0:S + 1], ALU.not_equal))
            nc.vector.tensor_scalar(newrow[:], newrow[:], NEG, None, ALU.mult).then_inc(s_new, 1)

            sparse = dve.value_load(flag[0:1, 0:1], min_val=0, max_val=1)
            with dve.If(sparse == 0):
                dve.wait_ge(s_c32, 1)
                nc.vector.tensor_copy(adj_f, adj_i[:]).then_inc(s_adjf, 1)
                dve.wait_ge(s_wacp, 1)
                nc.vector.tensor_copy(wa_wide[:], wa[:, 0:NH].unsqueeze(2).broadcast_to([P, NH, P])).then_inc(s_wide, 1)
                nc.vector.tensor_scalar(negm.rearrange("p q (j s) -> p q j s", j=Q),
                                        adj_i[:].rearrange("p q (s j) -> p q j s", j=Q), 0.0, NEG, ALU.is_le, ALU.mult)\
                    .then_inc(s_neg, 1)
                dve.wait_ge(s_xi, 16)
                with dve.Fori(0, NGROUP // NBUF) as it:
                    for b in range(NBUF):
                        dve.wait_ge(s_T[b], it * 16 + 16)
                        dve.wait_ge(s_agg, it * NBUF)
                        xb = x_il[:].rearrange("p q h -> p (q h)").unsqueeze(1).broadcast_to([P, G, Q * H])
                        nc.vector.tensor_tensor(prod[:, b % 2], T_buf[:, b], xb, ALU.mult).then_inc(s_prod, 1)

            dve.wait_ge(s_rz, 1)
            link(nc.vector.scalar_tensor_tensor(g_t[:], g_r[:], 1.0, hn_sb[:], ALU.add, ALU.mult))
            nc.vector.scalar_tensor_tensor(g_n[:], g_t[:], 0.5, ps_gate[2][:], ALU.mult, ALU.add).then_inc(s_npre, 1)
            dve.wait_ge(s_rz, 2)
            dve.wait_ge(s_nn, 1)
            link(nc.vector.tensor_tensor(g_t[:], x_sb[:], g_n[:], ALU.subtract))
            nc.vector.tensor_tensor(y[:], x_sb[:], g_n[:], ALU.add)
            link(nc.vector.scalar_tensor_tensor(g_t[:], g_z[:], 1.0, g_t[:], ALU.add, ALU.mult))
            link(nc.vector.scalar_tensor_tensor(y[:], g_t[:], 0.5, y[:], ALU.mult, ALU.add))

            def layernorm(src, dst, done, k):
                for q in range(Q):
                    t = nc.vector.bn_stats(st6[:, q], src[:, q])
                link(t)
                for q in range(Q):
                    t = nc.vector.bn_aggr(mv[:, q], st6[:, q])
                link(t)
                nc.vector.tensor_scalar(epsv[:], mv[:, :, 1], EPS, None, ALU.add).then_inc(s_var, 1)
                dve.wait_ge(s_rstd, k)
                for q in range(Q):
                    t = nc.vector.tensor_scalar(dst[:, q], src[:, q], mv[:, q, 0:1], rstd[:, q:q + 1],
                                                ALU.subtract, ALU.mult)
                t.then_inc(done, 1)

            layernorm(y, x1, s_x1, 1)
            dve.wait_ge(s_h, 2)
            nc.vector.tensor_copy(u_sb[:], ps_b[:, 0:Q * 2 * NH].rearrange("p (q n) -> p q n", q=Q)).then_inc(s_uc, 1)
            dve.wait_ge(s_uc, 1)
            with dve.If(sparse == 0):
                dve.wait_ge(s_v, 1)
                with dve.Fori(0, Q) as t:
                    at = [0]
                    per = 5 + NH

                    def tlink(ins):
                        at[0] += 1
                        ins.then_inc(s_dd, 1)
                        dve.wait_ge(s_dd, t * per + at[0])

                    u_t = u_sb[:, bass.ds(t, 1), NH:2 * NH].rearrange("p a n -> p (a n)")
                    for n in range(NH):
                        ins = nc.vector.tensor_tensor(vm[:, n], ps_v[n][:].rearrange("p q h -> p (q h)"),
                                                      negm[:, bass.ds(t, 1)].rearrange("p a j -> p (a j)"), ALU.add)
                    tlink(ins)
                    tlink(nc.vector.tensor_reduce(vmax[:], vm, AX, ALU.max))
                    tlink(nc.vector.tensor_tensor(m1[:], vmax[:], u_t, ALU.add))
                    tlink(nc.vector.scalar_tensor_tensor(nmax[:], m1[:], SLOPE, m1[:], ALU.mult, ALU.max))
                    nc.vector.tensor_scalar(nmax[:], nmax[:], -1.0, None, ALU.mult)
                    for n in range(NH):
                        u_tn = u_sb[:, bass.ds(t, 1), NH + n:NH + n + 1].rearrange("p a n -> p (a n)")
                        tlink(nc.vector.tensor_scalar(vm[:, n], vm[:, n], u_tn, None, ALU.add))
                        nc.vector.scalar_tensor_tensor(e_sb[:, n], vm[:, n], SLOPE, vm[:, n], ALU.mult, ALU.max)\
                            .then_inc(s_e, 1)
                    for n in range(NH):
                        dve.wait_ge(s_pt, t * NH + n + 1)
                        nc.vector.tensor_copy(pT[:, n], ps_t[n % 2][:]).then_inc(s_ptc, 1)
                    dve.wait_ge(s_p, t * NH + NH)
                    nc.vector.reciprocal(rinv[:], rsum[:]).then_inc(s_ri, 1)
                    dve.wait_ge(s_ri, t + 1)
                    dve.wait_ge(s_att, t + 1)
                    tlink(nc.vector.tensor_tensor(hp[:, bass.ds(t, 1)].rearrange("p a (n d) -> p (a n) d", n=NH),
                                                  ps_b[:, 0:H].rearrange("p (n d) -> p n d", n=NH),
                                                  rinv[:].unsqueeze(2).broadcast_to([P, NH, D]), ALU.mult))
            with dve.Else():
                steps = [0]

                def slink(ins):
                    steps[0] += 1
                    ins.then_inc(s_ds, 1)
                    dve.wait_ge(s_ds, steps[0])

                slink(nc.vector.tensor_copy(uv3[:, :, :, 0], u_sb[:]))
                slink(nc.vector.tensor_tensor(uvres[:], u_sb[:], uv3[:, :, :, 0], ALU.subtract))
                slink(nc.vector.tensor_copy(uv3[:, :, :, 1], uvres[:]))
                nc.vector.tensor_tensor(uv3[:, :, :, 2], uvres[:], uv3[:, :, :, 1], ALU.subtract).then_inc(s_uv3, 1)
                dve.wait_ge(s_z, 1)
                slink(nc.vector.tensor_reduce(z_sb[:], z_bank[:, 0:NC * 3 * NH].rearrange("p (c n k) -> p c n k", c=NC, n=NH),
                                              AX, ALU.add))
                nc.vector.scalar_tensor_tensor(z2[:], z_sb[:], SLOPE, z_sb[:], ALU.mult, ALU.max).then_inc(s_zs, 1)
                for b in range(NB):
                    dve.wait_ge(s_zT, b + 1)
                    first = 0.0 if b == 0 else zmax_f[:, b * BS - 1:b * BS]
                    slink(nc.vector.tensor_tensor_scan(zmax_f[:, batch(b)], newrow[:, batch(b)], zT_bank[b][0:NH, 0:BS],
                                                       first, ALU.add, ALU.max))
                nc.vector.tensor_tensor_scan(zmax[:, ::-1], newrow[:, S:0:-1], zmax_f[:, ::-1],
                                             0.0, ALU.add, ALU.max).then_inc(s_zm, 1)
                dve.wait_ge(s_mT, 1)
                nc.vector.tensor_tensor(z_sb[:], z2[:], z_bank[:, 0:NC * NH].rearrange("p (c n) -> p c n", c=NC),
                                        ALU.subtract).then_inc(s_ze, 1)
                dve.wait_ge(s_pe, 1)
                for b in range(NB):
                    cs = slice(b * B, (b + 1) * B)
                    nc.vector.tensor_copy(vals[:, cs, H:H + NH], p_edge[:, cs])
                    dve.wait_ge(s_hg, b + 1)
                    nc.vector.tensor_tensor(vals[:, cs, 0:H].rearrange("p c (n d) -> p c n d", n=NH),
                                            hg_bank[b][:, 0:BS].rearrange("p (c n d) -> p c n d", c=B, n=NH),
                                            p_edge[:, cs].unsqueeze(3).broadcast_to([P, B, NH, D]), ALU.mult)\
                        .then_inc(s_vals, 1)
                dve.wait_ge(s_num, 1)
                for k in range(2):
                    t = nc.vector.reciprocal(dinv[:, 2 * k:2 * k + 2], num_bank[k][:, :, H:H + NH])
                slink(t)
                for k in range(2):
                    t = nc.vector.tensor_tensor(hp[:, 2 * k:2 * k + 2].rearrange("p q (n d) -> p q n d", n=NH),
                                                num_bank[k][:, :, 0:H].rearrange("p q (n d) -> p q n d", n=NH),
                                                dinv[:, 2 * k:2 * k + 2].unsqueeze(3).broadcast_to([P, 2, NH, D]), ALU.mult)
                slink(t)
            link(nc.vector.tensor_tensor(y[:].rearrange("p n (q d) -> p n q d", q=Q),
                                         x1[:].rearrange("p n (q d) -> p n q d", q=Q),
                                         hp[:].rearrange("p q (n d) -> p n q d", n=NH), ALU.add))
            layernorm(y, out_sb, s_o, 2)


_INS = ["x", "adj", "L0_gnn_edge_table", "L0_gnn_w_ih", "L0_gnn_w_hh", "L0_gnn_b_ih", "L0_gnn_b_hh",
        "L1_gnn_W", "L1_gnn_a"]


def kernel(**inputs):
    import numpy as _np
    import concourse.bacc as _bacc
    from concourse import mybir as _mybir
    from concourse.bass_utils import run_bass_kernel_spmd as _run

    nc = _bacc.Bacc("TRN2", target_bir_lowering=False, num_devices=1)
    arrays, args = {}, []
    for name in _INS:
        a = _np.ascontiguousarray(inputs[name])
        arrays[f"in_{name}"] = a
        args.append(nc.dram_tensor(f"in_{name}", a.shape, _mybir.dt.from_np(a.dtype), kind="ExternalInput").ap())
    out = nc.dram_tensor("out_0", inputs["x"].shape, F32, kind="ExternalOutput").ap()
    build_gnn(nc, *args, out)
    r = _run(nc, [arrays], core_ids=[0])
    return r.results[0]["out_0"]
```

```python
from contextlib import ExitStack

import concourse.bass as bass
from concourse import mybir

F32 = mybir.dt.float32
F16 = mybir.dt.float16
BF16 = mybir.dt.bfloat16
U32 = mybir.dt.uint32
I32 = mybir.dt.int32
ALU = mybir.AluOpType
ACT = mybir.ActivationFunctionType

P = 128
EPS = 1e-5
SLOPE = 0.2
NEG = -1e30
POS_MAX = 2040.0
AX = mybir.AxisListType.X


def build_gnn(nc, x, adj, edge_table, w_ih, w_hh, b_ih, b_hh, w_gat, a_gat, out):
    N, H = x.shape
    Q = N // P
    NH, _, D = w_gat.shape
    G = 4
    NBUF = 2
    NC = 9
    B = 3
    CPE = 5
    NB = NC // B
    S = NC * P
    BROWS = 96
    BS = B * P
    NGROUP = N // G
    AHEAD = 2
    assert H == P and NH * D == H and Q == 4

    with ExitStack() as ctx:
        def sb(name, shape, dt=F32):
            return ctx.enter_context(nc.sbuf_tensor(name, shape, dt))

        def ps(name, shape, dt=F32):
            return ctx.enter_context(nc.psum_tensor(name, shape, dt))

        def sem(name):
            return ctx.enter_context(nc.semaphore(name))

        x_sb = sb("x_sb", [P, Q, H])
        x_half = sb("x_half", [P, Q, H])
        x_il = sb("x_il", [P, Q, H])
        adj_i = sb("adj_i", [P, Q, N], I32)
        wih_sb = sb("wih_sb", [P, 3, H])
        whh_sb = sb("whh_sb", [P, 3, H])
        bias4 = sb("bias4", [BROWS, 4, H])
        bias_hh = sb("bias_hh", [BROWS, 2, H])
        bias_lo = sb("bias_lo", [BROWS, 4, H])
        bias_mid = sb("bias_mid", [BROWS, 4, H], BF16)
        bias3 = sb("bias3", [BROWS, 4, H], BF16)
        wcat = sb("wcat", [P, H + 2 * NH])
        a_col = sb("a_col", [P, 2])
        ident = sb("ident", [P, P])
        headmask = sb("headmask", [P, NH])
        adj_f_all = sb("adj_f", [P, Q, N])
        adj_f = adj_f_all[:]
        negm_all = sb("negm", [P, Q, N])
        negm = negm_all[:]
        adjT = sb("adjT", [P, max(Q * N, NC * N // 2)])
        rowhot_num = adjT[:].bitcast(F16)[:, 0:NC * N].rearrange("p (c q i) -> p c q i", c=NC, q=Q)
        adjT = adjT[:, 0:Q * N].rearrange("p (j i) -> p j i", j=Q)
        xT = sb("xT", [P, Q, P])
        wT = sb("wT", [P, 7, P])
        a_bd = sb("a_bd", [P, 2, NH])
        wa = wcat[:, H:H + 2 * NH]
        wa_wide = sb("wa_wide", [P, NH, P])
        T_buf = sb("T_buf", [P, NBUF, G, Q * H])
        sparse_area = T_buf[:].rearrange("p b g f -> p (b g f)")
        vals = sparse_area[:, 0:NC * (H + NH)].rearrange("p (c f) -> p c f", c=NC)
        zmax_f = sparse_area[0:NH, NC * (H + NH):NC * (H + NH) + S]
        zmax = sparse_area[0:NH, NC * (H + NH) + S:NC * (H + NH) + 2 * S]
        prod = sb("prod", [P, 2, G, Q * H])
        vals3 = prod[:].rearrange("p b g f -> p (b g f)").bitcast(BF16)[:, 0:3 * NC * (H + NH)]\
            .rearrange("p (k c f) -> p k c f", k=3, c=NC)
        acol = sb("acol", [P, 2, Q, Q])
        aggT = sb("aggT", [P, Q, P])
        warm = sb("warm", [1, 1])
        iota_s = sb("iota_s", [P, S], F16)
        iota_il = sb("iota_il", [P, Q, P], F16)
        node_id = sb("node_id", [P, Q])
        slot_half = sb("slot_half", [P, NC])
        upper16 = sb("upper16", [P, P], F16)
        ones16 = sb("ones16", [P, P], F16)
        ident16 = sb("ident16", [P, P], F16)
        x1sum = sb("x1sum", [P, 1])
        ones_f = sb("ones_f", [P, P])
        x3 = sb("x3", [P, 3, Q, H], BF16)
        y = sb("y", [P, Q, H])
        xres = y
        ones_adj = sb("ones_adj", [P, N], F16)
        prefix = sb("prefix", [P, Q, N], F16)
        deg_pad = sb("deg_pad", [P, 2 * Q], F16)
        deg16 = deg_pad[:, Q:2 * Q]
        sums = sb("sums", [P, 2])
        totals = sb("totals", [P, 2])
        same = sb("same", [P, 1])
        flag = sb("flag", [P, 1], I32)
        base = sb("base", [P, Q])
        cum = sb("cum", [P, Q])
        pos = sb("pos", [P, Q, N], F16)
        is_ge = sb("is_ge", [P, Q, BS], F16)
        is_lt = sb("is_lt", [P, Q, BS], F16)
        rowhot = sb("rowhot", [P, Q, S], F16)
        colhot = sb("colhot", [P, Q, S], F16)
        rowhotT = sb("rowhotT", [P, NC, N])
        sgn = sb("sgn", [P, 2, N], F16)
        cnt = sb("cnt", [P, NC])
        row1 = sb("row1", [P, NC])
        row0 = sb("row0", [P, NC])
        slot_id = sb("slot_id", [P, NC])
        rowoff = sb("rowoff", [P, NC])
        eidx_f = sb("eidx_f", [P, NC])
        sidx_f = sb("sidx_f", [P, NC])
        sidx = sb("sidx", [P, NC], U32)
        eidx = sb("eidx", [P, NC], U32)
        jcast = sb("jcast", [P, NC, P], F16)
        rcast = sb("rcast", [P, NC, NH], F16)
        jrow = sb("jrow", [P, S], F16)
        rrow = sb("rrow", [NH, S + 2])
        newrow = sb("newrow", [NH, S + 1])
        edge = sb("edge", [P, NC, H])
        xg = sb("xg", [P, NC, H])
        eprod = sb("eprod", [P, NC, H])
        hn_sb = sb("hn_sb", [P, Q, H])
        empty = sb("empty", [P, Q])
        erow = sb("erow", [1, Q, P])
        meanrow = sb("meanrow", [1, H + NH])
        uvres = sb("uvres", [P, Q, 2 * NH])
        uv3 = sb("uv3", [P, Q, 2 * NH, 3], BF16)
        z_sb = sb("z_sb", [P, NC, NH])
        z2 = sb("z2", [P, NC, NH])
        p_edge = sb("p_edge", [P, NC, NH])
        dinv = sb("dinv", [P, Q, NH])
        g_r = sb("g_r", [P, Q, H])
        g_z = sb("g_z", [P, Q, H])
        g_n = sb("g_n", [P, Q, H])
        g_t = sb("g_t", [P, Q, H])
        g_t2 = sb("g_t2", [P, Q, H])
        st6 = sb("st6", [P, Q, 2, 6])
        mv = sb("mv", [P, Q, 2])
        epsv = sb("epsv", [P, Q])
        mhalf = sb("mhalf", [P, Q])
        rstd = sb("rstd", [P, Q])
        x1 = sb("x1", [P, Q, H])
        x1T = sb("x1T", [P, Q, P])
        x1T_il = x1T[:].rearrange("h t p -> h (t p)").rearrange("h (s q) -> h q s", q=Q)
        h3 = sb("h3", [P, 3, Q, H], BF16)
        hres = y
        h_sb = g_t
        u_sb = sb("u_sb", [P, Q, 2 * NH])
        vm = T_buf[:].rearrange("p b g f -> p (b g f)")[:, 0:NH * N].rearrange("p (n j) -> p n j", n=NH)
        vmax = sb("vmax", [P, NH])
        m1 = sb("m1", [P, NH])
        nmax = sb("nmax", [P, NH])
        e_sb = T_buf[:].rearrange("p b g f -> p (b g f)")[:, NH * N:2 * NH * N].rearrange("p (n j) -> p n j", n=NH)
        p_sb = prod[:].rearrange("p b g f -> p (b g f)")[:, 0:NH * N].rearrange("p (n j) -> p n j", n=NH)
        rsum = sb("rsum", [P, NH])
        rinv = sb("rinv", [P, NH])
        pT = prod[:].rearrange("p b g f -> p (b g f)")[:, NH * N:2 * NH * N].rearrange("p (n q i) -> p n q i", n=NH, q=Q)
        hp = g_t2
        out_sb = g_n

        ps_gate = [ps(f"ps_gate{k}", [P, Q, H]) for k in range(4)]
        ps_v = ps_gate
        ps_t = [ps(f"ps_t{k}", [P, 4, P]) for k in range(2)]
        ps_a = ps("ps_a", [P, Q, P])
        ps_b = ps("ps_b", [P, 512])
        sel_bank = [ps_t[k][:].rearrange("p q i -> p (q i)") for k in range(2)]
        xg_bank = [ps_a[:].rearrange("p q i -> p (q i)"), sel_bank[0]]
        rrow_bank = sel_bank + [xg_bank[0]]
        proj_bank = [t.rearrange("p q f -> p (q f)")[:, 0:2 * (H + 2 * NH)].rearrange("p (q f) -> p q f", q=2)
                     for t in (ps_a[:], ps_gate[1][:])]
        agg_bank = ps_b[:]
        z_bank = ps_gate[0][:].rearrange("p q h -> p (q h)")
        mean_bank = ps_b[0:1, 0:H]
        zT_bank = [ps_b[:], ps_a[:].rearrange("p q i -> p (q i)"), ps_gate[1][:].rearrange("p q h -> p (q h)")]
        hg_bank = [ps_gate[2][:].rearrange("p q h -> p (q h)"), ps_gate[3][:].rearrange("p q h -> p (q h)"),
                   ps_gate[1][:].rearrange("p q h -> p (q h)")]
        num_bank = [ps_t[k][:].rearrange("p q i -> p (q i)")[:, 0:2 * (H + NH)].rearrange("p (q f) -> p q f", q=2)
                    for k in range(2)]
        row_bank = ps_gate[3][:].rearrange("p q h -> p (q h)")
        ps_ab = [ps_a[:].rearrange("p q i -> p (q i)"), ps_b[:]]

        s_x = sem("s_x"); s_xi = sem("s_xi"); s_adj = [sem(f"s_adj{q}") for q in range(Q)]; s_w = sem("s_w")
        s_whh = sem("s_whh"); s_bias = sem("s_bias"); s_ac = sem("s_ac")
        s_bz = sem("s_bz"); s_c16 = sem("s_c16"); s_iota = sem("s_iota"); s_const = sem("s_const")
        s_slot = sem("s_slot"); s_il = sem("s_il"); s_bsum = sem("s_bsum"); s_bhi = sem("s_bhi")
        s_bres = sem("s_bres"); s_bmid = sem("s_bmid"); s_bias3 = sem("s_bias3"); s_x3 = sem("s_x3")
        s_abd = sem("s_abd"); s_wa = sem("s_wa"); s_wacp = sem("s_wacp")
        s_tp = sem("s_tp"); s_tc = sem("s_tc"); s_er = sem("s_er"); s_erc = sem("s_erc")
        s_sum = sem("s_sum"); s_sq = sem("s_sq"); s_base = sem("s_base"); s_basec = sem("s_basec")
        s_tot = sem("s_tot"); s_flag = sem("s_flag"); s_emp = sem("s_emp")
        s_row = sem("s_row"); s_pos = sem("s_pos"); s_sel = sem("s_sel"); s_cnt = sem("s_cnt"); s_idx = sem("s_idx")
        s_sidx = sem("s_sidx"); s_cast = sem("s_cast"); s_rT = sem("s_rT"); s_rnum = sem("s_rnum")
        s_jr = sem("s_jr"); s_jrc = sem("s_jrc"); s_rr = sem("s_rr"); s_rrc = sem("s_rrc"); s_col = sem("s_col")
        s_new = sem("s_new")
        s_edge = [sem(f"s_edge{c}") for c in range(NC)]; s_xs = [sem(f"s_xs{c}") for c in range(NC)]
        s_xg = sem("s_xg"); s_xgc = sem("s_xgc"); s_ep = sem("s_ep"); s_aggs = sem("s_aggs"); s_aggT = sem("s_aggT")
        s_hn = sem("s_hn"); s_hnc = sem("s_hnc"); s_gate = sem("s_gate"); s_rz = sem("s_rz"); s_npre = sem("s_npre")
        s_nn = sem("s_nn"); s_var = sem("s_var"); s_rstd = sem("s_rstd"); s_x1 = sem("s_x1"); s_o = sem("s_o")
        s_h = sem("s_h"); s_x1T = sem("s_x1T"); s_uc = sem("s_uc"); s_uv3 = sem("s_uv3"); s_h3 = sem("s_h3")
        s_hres = sem("s_hres"); s_mean = sem("s_mean"); s_meanc = sem("s_meanc")
        s_z = sem("s_z"); s_zs = sem("s_zs"); s_zT = sem("s_zT"); s_zm = sem("s_zm"); s_mT = sem("s_mT")
        s_ze = sem("s_ze"); s_pe = sem("s_pe"); s_hg = sem("s_hg"); s_vals = sem("s_vals"); s_vhi = sem("s_vhi")
        s_vres = sem("s_vres"); s_vmid = sem("s_vmid"); s_v3 = sem("s_v3"); s_num = sem("s_num")
        s_rcp = sem("s_rcp")
        s_T = [sem(f"s_T{b}") for b in range(NBUF)]; s_adjf = sem("s_adjf"); s_adjTp = sem("s_adjTp")
        s_adjT = sem("s_adjT"); s_prod = sem("s_prod"); s_acol = sem("s_acol"); s_agg = sem("s_agg")
        s_aggc = sem("s_aggc"); s_wide = sem("s_wide"); s_neg = sem("s_neg"); s_hc = sem("s_hc"); s_v = sem("s_v")
        s_e = sem("s_e"); s_p = sem("s_p"); s_pt = sem("s_pt"); s_ptc = sem("s_ptc"); s_att = sem("s_att")
        s_ri = sem("s_ri")
        s_dv = sem("s_dv"); s_ds = sem("s_ds"); s_dd = sem("s_dd")
        s_out = sem("s_out")

        x_v = x.rearrange("(p q) h -> p q h", q=Q)
        out_v = out.rearrange("(t p) h -> p t h", p=P)
        adj_v = adj.rearrange("(p q) j -> p q j", q=Q)
        T_v = edge_table.rearrange("(i p q) h -> i p (q h)", p=P, q=Q)

        block = ctx.enter_context(nc.Block())

        def batch(b):
            return slice(b * BS, (b + 1) * BS)

        @block.sync
        def _(sp):
            for q in range(Q):
                sp.dma_start(adj_i[:, q], adj_v[:, q]).then_inc(s_adj[q], 16)
            sp.dma_start(x_sb[:], x.rearrange("(t p) h -> p t h", p=P)).then_inc(s_x, 16)
            sp.dma_start(whh_sb[:], w_hh.rearrange("(g p) h -> p g h", p=P)).then_inc(s_whh, 16)
            sp.dma_start(wih_sb[:], w_ih.rearrange("(g p) h -> p g h", p=P)).then_inc(s_w, 16)
            sp.dma_start(wcat[:, 0:H].rearrange("p (n d) -> p n d", n=NH), w_gat.rearrange("n p d -> p n d"))\
                .then_inc(s_w, 16)
            sp.dma_start(x_il[:], x_v).then_inc(s_xi, 16)
            with nc.allow_non_contiguous_dma(reason="256 attention weights"):
                for n in range(NH):
                    sp.dma_start(a_col[n * D:(n + 1) * D, :],
                                 a_gat[n, :, 0].rearrange("(k d) -> d k", k=2)).then_inc(s_ac, 16)
            sp.wait_ge(s_flag, 1)
            sparse = sp.value_load(flag[0:1, 0:1], min_val=0, max_val=1)
            with sp.If(sparse == 0):
                for b in range(NBUF):
                    sp.dma_start(T_buf[:, b], T_v[b * G:(b + 1) * G].rearrange("i p f -> p i f")).then_inc(s_T[b], 16)
                with sp.Fori(0, NGROUP // NBUF - 1) as it:
                    for b in range(NBUF):
                        sp.wait_ge(s_prod, it * NBUF + b + 1)
                        src = T_v[bass.ds((it * NBUF + b + NBUF) * G, G)].rearrange("i p f -> p i f")
                        sp.dma_start(T_buf[:, b], src).then_inc(s_T[b], 16)
            for k in range(2):
                sp.wait_ge(s_o, 2 * k + 2)
                sp.dma_start(out_v[:, 2 * k:2 * k + 2], out_sb[:, 2 * k:2 * k + 2]).then_inc(s_out, 16)
            sp.wait_ge(s_out, 32)

        @block.gpsimd
        def _(pool):
            nc.gpsimd.memset(ident[:], 0.0).then_inc(s_const, 1)
            nc.gpsimd.memset(headmask[:], 1.0).then_inc(s_const, 1)
            nc.gpsimd.memset(upper16[:], 0.0).then_inc(s_const, 1)
            nc.gpsimd.iota(iota_s[:], [[1, S]], base=0, channel_multiplier=0,
                           allow_small_or_imprecise_dtypes=True).then_inc(s_iota, 1)
            nc.gpsimd.iota(node_id[:], [[1, Q]], base=0, channel_multiplier=Q,
                           allow_small_or_imprecise_dtypes=True).then_inc(s_iota, 1)
            nc.gpsimd.iota(slot_id[:], [[P, NC]], base=0, channel_multiplier=1,
                           allow_small_or_imprecise_dtypes=True).then_inc(s_iota, 1)
            pool.wait_ge(s_const, 3)
            nc.gpsimd.affine_select(out=ident[:], in_=ident[:], compare_op=ALU.not_equal, fill=1.0, base=0,
                                    pattern=[[-1, P]], channel_multiplier=1).then_inc(s_const, 1)
            nc.gpsimd.affine_select(out=headmask[:], in_=headmask[:], compare_op=ALU.is_ge, fill=0.0, base=0,
                                    pattern=[[-D, NH]], channel_multiplier=1).then_inc(s_const, 1)
            nc.gpsimd.affine_select(out=upper16[:], in_=upper16[:], compare_op=ALU.is_ge, fill=1.0, base=0,
                                    pattern=[[-1, P]], channel_multiplier=1).then_inc(s_const, 1)
            pool.wait_ge(s_const, 6)
            nc.gpsimd.affine_select(out=headmask[:], in_=headmask[:], compare_op=ALU.is_ge, fill=0.0, base=D - 1,
                                    pattern=[[D, NH]], channel_multiplier=-1).then_inc(s_const, 1)
            pool.wait_ge(s_bias, 48)
            nc.gpsimd.tensor_tensor(bias4[:, 0:2], bias4[:, 0:2], bias_hh[:], ALU.add).then_inc(s_bsum, 1)
            pool.wait_ge(s_bhi, 1)
            nc.gpsimd.tensor_tensor(bias_lo[:], bias4[:], bias3[:], ALU.subtract).then_inc(s_bres, 1)
            pool.wait_ge(s_bres, 1)
            pool.wait_ge(s_xi, 16)
            nc.gpsimd.tensor_copy(x3[:, 0], x_il[:]).then_inc(s_x3, 1)
            pool.wait_ge(s_x3, 1)
            pool.wait_ge(s_bmid, 2)
            nc.gpsimd.tensor_tensor(bias3[64:96], bias_lo[64:96], bias_mid[64:96], ALU.subtract).then_inc(s_bias3, 1)
            pool.wait_ge(s_bias3, 1)
            nc.gpsimd.tensor_tensor(xres[:], x_il[:], x3[:, 0], ALU.subtract).then_inc(s_x3, 1)
            pool.wait_ge(s_x3, 2)
            nc.gpsimd.tensor_copy(x3[:, 1], xres[:]).then_inc(s_x3, 1)
            pool.wait_ge(s_x3, 3)
            nc.gpsimd.tensor_tensor(x3[:, 2], xres[:], x3[:, 1], ALU.subtract).then_inc(s_x3, 1)
            for b in range(NB):
                pool.wait_ge(s_idx, b + 1)
                for c in range(b * B, (b + 1) * B):
                    nc.gpsimd.indirect_dma_start(
                        out=edge[:, c], out_offset=None, in_=edge_table,
                        in_offset=bass.IndirectOffsetOnAxis(ap=eidx[:, c:c + 1], axis=0)).then_inc(s_edge[c], 16)
                if (b + 1) * B > CPE:
                    pool.wait_ge(s_sidx, b - CPE // B + 1)
                    for c in range(max(b * B, CPE), (b + 1) * B):
                        nc.gpsimd.indirect_dma_start(
                            out=xg[:, c], out_offset=None, in_=x,
                            in_offset=bass.IndirectOffsetOnAxis(ap=sidx[:, c:c + 1], axis=0)).then_inc(s_xs[c], 16)
            pool.wait_ge(s_flag, 1)
            sparse = pool.value_load(flag[0:1, 0:1], min_val=0, max_val=1)
            with pool.If(sparse == 0):
                pool.wait_ge(s_adjT, Q)
                with pool.Fori(0, NGROUP // 2) as it:
                    for par in range(2):
                        pool.wait_ge(s_agg, it * 2 + AHEAD)
                        src = adjT.rearrange("p j (q i) -> p j q i", q=Q)[:, :, :, bass.ds(it * 2 + par, 1)]
                        nc.gpsimd.tensor_copy(acol[:, par].unsqueeze(3), src).then_inc(s_acol, 1)
            for k in range(2):
                pool.wait_ge(s_var, k + 1)
                nc.gpsimd.tensor_tensor(rstd[:], epsv[:], mhalf[:], ALU.pow).then_inc(s_rstd, 1)

        @block.scalar
        def _(act):
            act.wait_ge(s_bz, 3)
            with nc.allow_non_contiguous_dma(reason="biases, three times"):
                act.dma_start(bias4[0:BROWS:32, 0:3], b_ih.rearrange("(a g h) -> a g h", a=1, g=3).broadcast_to([3, 3, H]))\
                    .then_inc(s_bias, 16)
                act.dma_start(bias_hh[0:BROWS:32], b_hh[0:2 * H].rearrange("(a g h) -> a g h", a=1, g=2)
                              .broadcast_to([3, 2, H])).then_inc(s_bias, 16)
                act.dma_start(bias4[0:BROWS:32, 3], b_hh[2 * H:3 * H].rearrange("(a h) -> a h", a=1)
                              .broadcast_to([3, H])).then_inc(s_bias, 16)
            nc.scalar.activation(warm[:], warm[:], ACT.Tanh)
            for q in range(Q):
                act.wait_ge(s_adj[q], 16)
            nc.scalar.activation(negm, adj_i[:], ACT.Square, accum_out=sums[:, 0:1]).then_inc(s_sq, 1)
            act.wait_ge(s_bsum, 1)
            nc.scalar.copy(bias3[:], bias4[:]).then_inc(s_bhi, 1)
            act.wait_ge(s_tp, 1)
            nc.scalar.copy(xT[:], ps_t[0][:]).then_inc(s_tc, 1)
            act.wait_ge(s_tp, 2)
            nc.scalar.copy(wT[:, 4:7], ps_t[1][:, 0:3]).then_inc(s_tc, 1)
            act.wait_ge(s_bres, 1)
            nc.scalar.copy(bias_mid[64:96], bias_lo[64:96]).then_inc(s_bmid, 1)
            nc.scalar.copy(bias3[32:64], bias_lo[32:64]).then_inc(s_bmid, 1)
            act.wait_ge(s_slot, 1)

            def count(b):
                for c in range(b * B, (b + 1) * B):
                    act.wait_ge(s_sel, c + 1)
                    nc.scalar.activation(sgn[:, c % 2, 0:N - 1], sel_bank[c % 2][:, 0:N - 1], ACT.Sign, scale=-1.0,
                                         bias=slot_half[:, c:c + 1], accum_out=cnt[:, c:c + 1])
                    nc.scalar.copy(row1[:, c:c + 1], sel_bank[c % 2][:, N - 1:N]).then_inc(s_cnt, 1)

            def keep_jrow(b):
                act.wait_ge(s_jr, b + 1)
                nc.scalar.copy(jrow[:, batch(b)], row_bank[:, 0:BS]).then_inc(s_jrc, 1)

            def keep_xg(b):
                act.wait_ge(s_xg, b + 1)
                n = min(B, CPE - b * B)
                nc.scalar.copy(xg[:, b * B:b * B + n].rearrange("p c h -> p (c h)"), xg_bank[b][:, 0:n * P])\
                    .then_inc(s_xgc, 1)

            count(0)
            act.wait_ge(s_hn, 1)
            nc.scalar.copy(hn_sb[:], ps_gate[3][:]).then_inc(s_hnc, 1)
            count(1)
            keep_jrow(0)
            act.wait_ge(s_tp, 3)
            nc.scalar.copy(wT[:, 0:4], ps_a[:]).then_inc(s_tc, 1)
            count(2)
            act.wait_ge(s_wa, 1)
            nc.scalar.copy(wa, ps_b[:, 0:2 * NH]).then_inc(s_wacp, 1)
            keep_jrow(1)
            keep_xg(0)
            keep_xg(1)
            keep_jrow(2)
            act.wait_ge(s_aggs, 1)
            for k in range(2):
                nc.scalar.copy(aggT[:, 2 * k:2 * k + 2].rearrange("h t p -> h (t p)"),
                               agg_bank[:, 2 * k * P:(2 * k + 2) * P]).then_inc(s_aggT, 1)
            sparse = act.value_load(flag[0:1, 0:1], min_val=0, max_val=1)
            with act.If(sparse == 0):
                act.wait_ge(s_rnum, NC)
                for j in range(Q):
                    act.wait_ge(s_adjTp, j + 1)
                    nc.scalar.copy(adjT[:, j], ps_t[j % 2][:].rearrange("p q i -> p (q i)")).then_inc(s_adjT, 1)
                nc.scalar.copy(aggT[:, Q - 1, 0:1], ident[:, 0:1]).then_inc(s_aggc, AHEAD)
                with act.Fori(0, NGROUP // 2) as it:
                    for par in range(2):
                        act.wait_ge(s_agg, it * 2 + par + 1 + AHEAD)
                        dst = aggT[:].rearrange("h t p -> h (t p)")[:, bass.ds((it * 2 + par) * G, G)]
                        nc.scalar.copy(dst, ps_ab[par][:, 0:G]).then_inc(s_aggc, 1)
            act.wait_ge(s_gate, 1)
            nc.scalar.activation(g_r[:], ps_gate[0][:], ACT.Tanh, scale=0.5).then_inc(s_rz, 1)
            act.wait_ge(s_gate, 3)
            nc.scalar.activation(g_z[:], ps_gate[1][:], ACT.Tanh, scale=0.5).then_inc(s_rz, 1)
            act.wait_ge(s_npre, 1)
            nc.scalar.activation(g_n[:], g_n[:], ACT.Tanh).then_inc(s_nn, 1)
            for b in range(NB):
                act.wait_ge(s_rr, b + 1)
                nc.scalar.copy(rrow[:, 1 + b * BS:1 + (b + 1) * BS], rrow_bank[b][0:NH, 0:BS]).then_inc(s_rrc, 1)
            act.wait_ge(s_er, 1)
            nc.scalar.copy(erow[:].rearrange("a q p -> a (q p)"), row_bank[0:1, :]).then_inc(s_erc, 1)
            act.wait_ge(s_h, 1)
            nc.scalar.activation(x1T[:], ps_t[0][:], ACT.Identity, accum_out=x1sum[:]).then_inc(s_x1T, 1)
            with act.If(sparse == 0):
                act.wait_ge(s_uc, 1)
                for k in range(2):
                    t = nc.scalar.copy(h_sb[:, 2 * k:2 * k + 2], proj_bank[k][:, :, 0:H])
                t.then_inc(s_hc, 1)
                with act.Fori(0, Q) as t:
                    for n in range(NH):
                        act.wait_ge(s_e, t * NH + n + 1)
                        nc.scalar.activation(p_sb[:, n], e_sb[:, n], ACT.Exp, bias=nmax[:, n:n + 1],
                                             accum_out=rsum[:, n:n + 1]).then_inc(s_p, 1)
            with act.Else():
                act.wait_ge(s_mean, 1)
                nc.scalar.mul(meanrow[:, 0:H], mean_bank, 1.0 / N).then_inc(s_meanc, 1)
                act.wait_ge(s_uc, 1)
                for k in range(2):
                    t = nc.scalar.copy(h3[:, 0, 2 * k:2 * k + 2], proj_bank[k][:, :, 0:H])
                t.then_inc(s_h3, 1)
                act.wait_ge(s_hres, 1)
                nc.scalar.copy(h3[:, 1], hres[:]).then_inc(s_h3, 1)
                act.wait_ge(s_ze, 1)
                nc.scalar.activation(p_edge[:], z_sb[:], ACT.Exp).then_inc(s_pe, 1)
                for b in range(NB):
                    cs = slice(b * B, (b + 1) * B)
                    act.wait_ge(s_vals, b + 1)
                    nc.scalar.copy(vals3[:, 0, cs], vals[:, cs]).then_inc(s_vhi, 1)
                    act.wait_ge(s_vres, b + 1)
                    nc.scalar.copy(vals3[:, 1, cs], vals[:, cs]).then_inc(s_vmid, 1)

        @block.tensor
        def _(pe):
            pe.wait_ge(s_const, 6)
            pe.wait_ge(s_c16, 3)
            pe.wait_ge(s_sum, 1)
            for n in range(Q):
                mm = nc.tensor.matmul(ps_b[:, 0:Q], upper16[:] if n == 0 else ones16[:], deg_pad[:, Q - n:2 * Q - n],
                                      start=(n == 0), stop=(n == Q - 1))
            mm.then_inc(s_base, 1)
            pe.wait_ge(s_x, 16)
            for q in range(Q):
                mm = nc.tensor.transpose(ps_t[0][:, q], x_sb[:, q], ident[:])
            mm.then_inc(s_tp, 1)
            pe.wait_ge(s_whh, 16)
            for g in range(3):
                mm = nc.tensor.transpose(ps_t[1][:, g], whh_sb[:, g], ident[:])
            mm.then_inc(s_tp, 1)

            def select(first, end):
                pe.wait_ge(s_pos, 1)
                for c in range(first, end):
                    pe.wait_ge(s_row, c + 1)
                    if c >= 2:
                        pe.wait_ge(s_cnt, c - 1)
                    for q in range(Q):
                        mm = nc.tensor.matmul(sel_bank[c % 2], rowhot[:, q, c * P:(c + 1) * P], pos[:, q],
                                              start=(q == 0), stop=(q == Q - 1))
                    mm.then_inc(s_sel, 1)

            def source_row(b):
                pe.wait_ge(s_cast, b + 1)
                if b == 0:
                    pe.wait_ge(s_hnc, 1)
                else:
                    pe.wait_ge(s_jrc, b)
                for c in range(b * B, (b + 1) * B):
                    mm = nc.tensor.matmul(row_bank[:, (c - b * B) * P:(c - b * B + 1) * P], jcast[:, c], ident16[:],
                                          start=True, stop=True)
                mm.then_inc(s_jr, 1)

            def target_row(b):
                for c in range(b * B, (b + 1) * B):
                    mm = nc.tensor.matmul(rrow_bank[b][0:NH, (c - b * B) * P:(c - b * B + 1) * P], rcast[:, c],
                                          ident16[:], start=True, stop=True)
                mm.then_inc(s_rr, 1)

            def source_features(b):
                pe.wait_ge(s_col, b + 1)
                pe.wait_ge(s_x3, 4)
                if b >= 1:
                    pe.wait_ge(s_cnt, NC)
                for c in range(b * B, min((b + 1) * B, CPE)):
                    for q in range(Q):
                        for k in range(3):
                            mm = nc.tensor.matmul(xg_bank[b][:, (c - b * B) * P:(c - b * B + 1) * P],
                                                  colhot[:, q, c * P:(c + 1) * P], x3[:, k, q],
                                                  start=(q == 0 and k == 0), stop=(q == Q - 1 and k == 2))
                mm.then_inc(s_xg, 1)

            def aggregate(b):
                for c in range(b * B, (b + 1) * B):
                    pe.wait_ge(s_rT, c + 1)
                    pe.wait_ge(s_ep, c + 1)
                    mm = nc.tensor.matmul(agg_bank, eprod[:, c], rowhotT[:, c], start=(c == 0), stop=(c == NC - 1))
                if b == NB - 1:
                    mm.then_inc(s_aggs, 1)

            def hidden(k, g):
                for q in range(Q):
                    nc.tensor.matmul(ps_gate[k][:, q], xT[:, q], wT[:, 4 + g], start=(q == 0), stop=False,
                                     skip_group_check=True)

            def add_bias(k):
                for q in range(Q):
                    mm = nc.tensor.matmul(ps_gate[k][:, q], ones16[0:BROWS], bias3[:, k], start=(k == 2 and q == 0),
                                          stop=(k == 3), skip_group_check=True)
                return mm

            pe.wait_ge(s_w, 32)
            for g in range(3):
                nc.tensor.transpose(ps_a[:, g], wih_sb[:, g], ident[:])
            nc.tensor.transpose(ps_a[:, 3], wcat[:, 0:H], ident[:]).then_inc(s_tp, 1)
            pe.wait_ge(s_tc, 2)
            hidden(0, 0)
            select(0, 1)
            hidden(1, 1)
            select(1, 2)
            hidden(3, 2)
            select(2, 3)
            pe.wait_ge(s_bmid, 2)
            pe.wait_ge(s_bias3, 1)
            add_bias(3).then_inc(s_hn, 1)
            select(B, 2 * B)
            source_row(0)
            pe.wait_ge(s_sq, 1)
            pe.wait_ge(s_basec, 1)
            nc.tensor.matmul(ps_b[:, 0:2], ones_f[:], sums[:], start=True, stop=True).then_inc(s_tot, 1)
            for k in range(3):
                add_bias(k)
            select(2 * B, NC)
            pe.wait_ge(s_tc, 3)
            pe.wait_ge(s_abd, 1)
            pe.wait_ge(s_flag, 1)
            nc.tensor.matmul(ps_b[:, 0:2 * NH], wT[:, 3], a_bd[:].rearrange("p k n -> p (k n)"),
                             start=True, stop=True).then_inc(s_wa, 1)
            source_row(1)
            source_features(0)
            source_features(1)
            source_row(2)
            pe.wait_ge(s_wacp, 1)
            aggregate(0)
            aggregate(1)
            aggregate(2)
            sparse = pe.value_load(flag[0:1, 0:1], min_val=0, max_val=1)
            with pe.If(sparse == 0):
                pe.wait_ge(s_adjf, 1)
                pe.wait_ge(s_aggT, 2)
                for j in range(Q):
                    if j >= 2:
                        pe.wait_ge(s_adjT, j - 1)
                    for q in range(Q):
                        src = adj_f[:, q].rearrange("p (s j) -> p j s", j=Q)[:, j]
                        mm = nc.tensor.transpose(ps_t[j % 2][:, q], src, ident[:])
                        if j == 0 and q == 0:
                            mm.then_inc(s_agg, AHEAD)
                    mm.then_inc(s_adjTp, 1)
                with pe.Fori(0, NGROUP // 2) as it:
                    for par in range(2):
                        pe.wait_ge(s_prod, it * 2 + par + 1)
                        pe.wait_ge(s_acol, it * 2 + par + 1)
                        pe.wait_ge(s_aggc, it * 2 + AHEAD)
                        for b in range(G):
                            for j in range(Q):
                                mm = nc.tensor.matmul(ps_ab[par][:, b:b + 1], prod[:, par, b, j * H:(j + 1) * H],
                                                      acol[:, par, j, b:b + 1], start=(j == 0), stop=(j == Q - 1))
                        mm.then_inc(s_agg, 1)
                pe.wait_ge(s_aggc, NGROUP + AHEAD)
            for k in (0, 2, 1):
                for q in range(Q):
                    if k == 0:
                        pe.wait_ge(s_aggT, q // 2 + 1)
                    mm = nc.tensor.matmul(ps_gate[k][:, q], aggT[:, q], wT[:, k], start=False, stop=True,
                                          skip_group_check=True)
                mm.then_inc(s_gate, 1)
            for b in range(NB):
                target_row(b)
            pe.wait_ge(s_emp, 1)
            for q in range(Q):
                mm = nc.tensor.transpose(row_bank[0:1, q * P:(q + 1) * P], empty[:, q:q + 1], ident[:])
            mm.then_inc(s_er, 1)
            pe.wait_ge(s_rrc, NB)
            for q in range(Q):
                pe.wait_ge(s_x1, q + 1)
                mm = nc.tensor.transpose(ps_t[0][:, q], x1[:, q], ident[:])
            mm.then_inc(s_h, 1)
            pe.wait_ge(s_x1T, 1)
            for q in range(Q):
                mm = nc.tensor.matmul(proj_bank[q // 2][:, q % 2], x1T_il[:, q], wcat[:], start=True, stop=True)
            mm.then_inc(s_h, 1)
            with pe.If(sparse == 0):
                pe.wait_ge(s_wide, 1)
                pe.wait_ge(s_uc, 1)
                pe.wait_ge(s_hc, 1)
                for n in range(NH):
                    mm = nc.tensor.matmul(ps_v[n][:], wa_wide[:, n], x1T_il, start=True, stop=True)
                mm.then_inc(s_v, 1)
                with pe.Fori(0, Q) as t:
                    for n in range(NH):
                        pe.wait_ge(s_p, t * NH + n + 1)
                        if n >= 2:
                            pe.wait_ge(s_ptc, t * NH + n - 1)
                        for j in range(Q):
                            mm = nc.tensor.transpose(ps_t[n % 2][:, j], p_sb[:, n, j * P:(j + 1) * P], ident[:])
                        mm.then_inc(s_pt, 1)
                        pe.wait_ge(s_ptc, t * NH + n + 1)
                        for j in range(Q):
                            mm = nc.tensor.matmul(ps_b[:, n * D:(n + 1) * D], pT[:, n, j], h_sb[:, j, n * D:(n + 1) * D],
                                                  start=(j == 0), stop=(j == Q - 1))
                    mm.then_inc(s_att, 1)
            with pe.Else():
                nc.tensor.matmul(mean_bank, x1sum[:], wcat[:, 0:H], start=True, stop=True).then_inc(s_mean, 1)

                def add_mean(k):
                    for q in range(2 * k, 2 * k + 2):
                        nc.tensor.matmul(num_bank[k][:, q % 2], erow[:, q], meanrow[:], start=(q % 2 == 0), stop=False,
                                         skip_group_check=True)

                pe.wait_ge(s_erc, 1)
                pe.wait_ge(s_meanc, 1)
                add_mean(0)
                pe.wait_ge(s_uv3, 1)
                for b in range(NB):
                    for c in range(b * B, (b + 1) * B):
                        at = z_bank[:, c * 3 * NH:(c + 1) * 3 * NH]
                        for q in range(Q):
                            nc.tensor.matmul(at, rowhot[:, q, c * P:(c + 1) * P],
                                             uv3[:, q, NH:2 * NH].rearrange("p n k -> p (n k)"),
                                             start=(q == 0), stop=False)
                        for q in range(Q):
                            mm = nc.tensor.matmul(at, colhot[:, q, c * P:(c + 1) * P],
                                                  uv3[:, q, 0:NH].rearrange("p n k -> p (n k)"),
                                                  start=False, stop=(q == Q - 1))
                mm.then_inc(s_z, 1)

                def gather_h(first, end):
                    for c in range(first, end):
                        out_c = hg_bank[c // B][:, (c % B) * P:(c % B + 1) * P]
                        for q in range(Q):
                            for k in range(3):
                                mm = nc.tensor.matmul(out_c, colhot[:, q, c * P:(c + 1) * P], h3[:, k, q],
                                                      start=(q == 0 and k == 0), stop=(q == Q - 1 and k == 2))
                    if end % B == 0:
                        mm.then_inc(s_hg, 1)

                pe.wait_ge(s_h3, 3)
                gather_h(0, 1)
                pe.wait_ge(s_zs, 1)
                for b in range(NB):
                    for c in range(b * B, (b + 1) * B):
                        mm = nc.tensor.transpose(zT_bank[b][0:NH, (c - b * B) * P:(c - b * B + 1) * P], z2[:, c], ident[:])
                    mm.then_inc(s_zT, 1)

                gather_h(1, B)
                add_mean(1)
                pe.wait_ge(s_zm, 1)
                for c in range(NC):
                    mm = nc.tensor.transpose(z_bank[:, c * NH:(c + 1) * NH], zmax[:, c * P:(c + 1) * P], ident[0:NH, 0:NH])
                mm.then_inc(s_mT, 1)
                gather_h(B, 2 * B)
                gather_h(2 * B, NC)
                pe.wait_ge(s_rnum, NC)

                def scatter(chunks, tiles):
                    for c in chunks:
                        pe.wait_ge(s_v3, c // B + 1)
                        for q in tiles:
                            for k in range(3):
                                mm = nc.tensor.matmul(num_bank[q // 2][:, q % 2], rowhot_num[:, c, q], vals3[:, k, c],
                                                      start=False, stop=(c == NC - 1 and k == 2), skip_group_check=True)
                    return mm

                scatter(range(NC - B), range(Q))
                for k in range(2):
                    scatter(range(NC - B, NC), range(2 * k, 2 * k + 2)).then_inc(s_num, 1)

        @block.vector
        def _(dve):
            chain = [0]

            def link(ins):
                chain[0] += 1
                ins.then_inc(s_dv, 1)
                dve.wait_ge(s_dv, chain[0])

            nc.vector.memset(bias4[:], 0.0).then_inc(s_bz, 1)
            nc.vector.memset(warm[:], 0.0).then_inc(s_bz, 1)
            nc.vector.memset(bias_hh[:], 0.0).then_inc(s_bz, 1)
            nc.vector.memset(ones_adj[:], 1.0).then_inc(s_c16, 1)
            nc.vector.memset(ones16[:], 1.0).then_inc(s_c16, 1)
            nc.vector.memset(ones_f[:], 1.0).then_inc(s_c16, 1)
            nc.vector.memset(deg_pad[:, 0:Q], 0.0)
            nc.vector.memset(mhalf[:], -0.5)
            nc.vector.memset(meanrow[:, H:H + NH], 1.0)
            nc.vector.memset(rrow[:, 0:1], -1.0)
            nc.vector.memset(rrow[:, S + 1:S + 2], -1.0)
            dve.wait_ge(s_c16, 1)
            for q in range(Q):
                dve.wait_ge(s_adj[q], 16)
                t = nc.vector.tensor_tensor_scan(prefix[:, q], ones_adj[:], adj_i[:, q], 0.0, ALU.mult, ALU.add)
            link(t)
            link(nc.vector.tensor_copy(deg16, prefix[:, :, N - 1]))
            nc.vector.tensor_reduce(sums[:, 1:2], deg16, AX, ALU.add).then_inc(s_sum, 1)
            nc.vector.tensor_scalar(empty[:], deg16, 0.0, None, ALU.is_equal).then_inc(s_emp, 1)
            dve.wait_ge(s_const, 7)
            nc.vector.tensor_copy(ident16[:], ident[:])
            dve.wait_ge(s_iota, 3)
            nc.vector.tensor_scalar(slot_half[:], slot_id[:], 0.5, None, ALU.add).then_inc(s_slot, 1)
            dve.wait_ge(s_base, 1)
            nc.vector.tensor_tensor(cum[:], ps_b[:, 0:Q], deg16, ALU.add)
            nc.vector.tensor_copy(base[:], ps_b[:, 0:Q]).then_inc(s_basec, 1)
            dve.wait_ge(s_basec, 1)

            def row_onehot(first, end):
                slots = slice(first * P, end * P)
                n = (end - first) * P
                if first > 0:
                    dve.wait_ge(s_row, first)
                for q in range(Q):
                    nc.vector.tensor_scalar(is_ge[:, q, 0:n], iota_s[:, slots], base[:, q:q + 1], None, ALU.is_ge)
                    t = nc.vector.tensor_scalar(is_lt[:, q, 0:n], iota_s[:, slots], cum[:, q:q + 1], None, ALU.is_lt)
                link(t)
                nc.vector.tensor_tensor(rowhot[:, :, slots], is_ge[:, :, 0:n], is_lt[:, :, 0:n], ALU.mult)\
                    .then_inc(s_row, end - first)

            row_onehot(0, 1)
            for q in range(Q):
                t = nc.vector.tensor_scalar(pos[:, q], prefix[:, q], base[:, q:q + 1], POS_MAX, ALU.add, ALU.min)
            link(t)
            nc.vector.tensor_scalar(pos[:, :, N - 1], node_id[:], 1.0, None, ALU.add).then_inc(s_pos, 1)
            row_onehot(1, B)
            dve.wait_ge(s_ac, 16 * NH)
            nc.vector.tensor_scalar(a_bd[:, 0], headmask[:], a_col[:, 0:1], None, ALU.mult)
            nc.vector.tensor_scalar(a_bd[:, 1], headmask[:], a_col[:, 1:2], None, ALU.mult).then_inc(s_abd, 1)

            def edge_index(b):
                cs = slice(b * B, (b + 1) * B)
                dve.wait_ge(s_cnt, (b + 1) * B)
                link(nc.vector.tensor_scalar(rowoff[:, cs], row1[:, cs], float(N), (N - 1) / 2 - N, ALU.mult, ALU.add))
                link(nc.vector.scalar_tensor_tensor(eidx_f[:, cs], cnt[:, cs], 0.5, rowoff[:, cs], ALU.mult, ALU.add))
                nc.vector.tensor_scalar(eidx[:, cs], eidx_f[:, cs], 0.0, float(N * N - 1), ALU.max, ALU.min)\
                    .then_inc(s_idx, 1)

            def source_and_target(b):
                cs = slice(b * B, (b + 1) * B)
                nc.vector.tensor_scalar(jcast[:, cs], cnt[:, cs].unsqueeze(2).broadcast_to([P, B, P]),
                                        0.5, (N - 1) / 2, ALU.mult, ALU.add)
                nc.vector.tensor_copy(rcast[:, cs], row1[:, cs].unsqueeze(2).broadcast_to([P, B, NH])).then_inc(s_cast, 1)
                if (b + 1) * B > CPE:
                    link(nc.vector.tensor_scalar(sidx_f[:, cs], cnt[:, cs], 0.5, (N - 1) / 2, ALU.mult, ALU.add))
                    nc.vector.tensor_scalar(sidx[:, cs], sidx_f[:, cs], 0.0, float(N - 1), ALU.max, ALU.min)\
                        .then_inc(s_sidx, 1)
                link(nc.vector.tensor_scalar(row0[:, cs], row1[:, cs], -1.0, None, ALU.add))

            def col_onehot(b):
                dve.wait_ge(s_jrc, b + 1)
                for q in range(Q):
                    t = nc.vector.tensor_scalar(colhot[:, q, batch(b)], jrow[:, batch(b)], node_id[:, q:q + 1], None,
                                                ALU.is_equal)
                t.then_inc(s_col, 1)

            def row_onehot_T(b):
                for c in range(b * B, (b + 1) * B):
                    nc.vector.tensor_scalar(rowhotT[:, c], iota_s[:, 0:N], row0[:, c:c + 1], None, ALU.is_equal)\
                        .then_inc(s_rT, 1)

            def products(b):
                if b * B < CPE:
                    dve.wait_ge(s_xgc, b + 1)
                for c in range(b * B, (b + 1) * B):
                    dve.wait_ge(s_edge[c], 16)
                    if c >= CPE:
                        dve.wait_ge(s_xs[c], 16)
                    nc.vector.tensor_tensor(eprod[:, c], edge[:, c], xg[:, c], ALU.mult).then_inc(s_ep, 1)

            row_onehot(B, 2 * B)
            edge_index(0)
            source_and_target(0)
            row_onehot(2 * B, NC)
            edge_index(1)
            source_and_target(1)
            col_onehot(0)
            dve.wait_ge(s_tot, 1)
            link(nc.vector.tensor_copy(totals[:], ps_b[:, 0:2]))
            link(nc.vector.tensor_tensor(same[:], totals[:, 0:1], totals[:, 1:2], ALU.is_equal))
            nc.vector.scalar_tensor_tensor(flag[:], totals[:, 1:2], float(S), same[:], ALU.is_le, ALU.mult)\
                .then_inc(s_flag, 1)
            row_onehot_T(0)
            edge_index(2)
            col_onehot(1)
            source_and_target(2)
            products(0)
            row_onehot_T(1)
            products(1)
            row_onehot_T(2)
            col_onehot(2)
            products(2)
            nc.vector.tensor_copy(iota_il[:], iota_s[:, 0:N].rearrange("s (p q) -> s q p", q=Q)).then_inc(s_il, 1)
            dve.wait_ge(s_il, 1)
            for c in range(NC):
                nc.vector.tensor_scalar(rowhot_num[:, c], iota_il[:],
                                        row0[:, c:c + 1], None, ALU.is_equal).then_inc(s_rnum, 1)
            nc.vector.tensor_scalar(x_half[:], x_sb[:], 0.5, None, ALU.mult)
            sparse = dve.value_load(flag[0:1, 0:1], min_val=0, max_val=1)
            with dve.If(sparse == 0):
                nc.vector.tensor_copy(adj_f, adj_i[:]).then_inc(s_adjf, 1)
                dve.wait_ge(s_wacp, 1)
                nc.vector.tensor_copy(wa_wide[:], wcat[:, H:H + NH].unsqueeze(2).broadcast_to([P, NH, P])).then_inc(s_wide, 1)
                nc.vector.tensor_scalar(negm.rearrange("p q (j s) -> p q j s", j=Q),
                                        adj_i[:].rearrange("p q (s j) -> p q j s", j=Q), 0.0, NEG, ALU.is_le, ALU.mult)\
                    .then_inc(s_neg, 1)
                dve.wait_ge(s_xi, 16)
                with dve.Fori(0, NGROUP // NBUF) as it:
                    for b in range(NBUF):
                        dve.wait_ge(s_T[b], it * 16 + 16)
                        dve.wait_ge(s_agg, it * NBUF + AHEAD)
                        xb = x_il[:].rearrange("p q h -> p (q h)").unsqueeze(1).broadcast_to([P, G, Q * H])
                        nc.vector.tensor_tensor(prod[:, b % 2], T_buf[:, b], xb, ALU.mult).then_inc(s_prod, 1)

            dve.wait_ge(s_rz, 1)
            link(nc.vector.scalar_tensor_tensor(g_t[:], g_r[:], 1.0, hn_sb[:], ALU.add, ALU.mult))
            dve.wait_ge(s_gate, 2)
            nc.vector.scalar_tensor_tensor(g_n[:], g_t[:], 0.5, ps_gate[2][:], ALU.mult, ALU.add).then_inc(s_npre, 1)
            dve.wait_ge(s_rz, 2)
            nc.vector.scalar_tensor_tensor(g_t2[:], g_z[:], 3.0, x_half[:], ALU.add, ALU.mult)
            dve.wait_ge(s_nn, 1)
            link(nc.vector.scalar_tensor_tensor(y[:], g_z[:], 1.0, g_n[:], ALU.subtract, ALU.mult))
            link(nc.vector.scalar_tensor_tensor(y[:], y[:], -0.5, g_t2[:], ALU.mult, ALU.add))

            def statistics(src, half, count):
                for q in range(Q):
                    for f in range(half, half + count):
                        t = nc.vector.bn_stats(st6[:, q, f], src[:, q, f * H // 2:(f + 1) * H // 2])
                return t

            def normalise(src, dst, done, k, link):
                for q in range(Q):
                    t = nc.vector.bn_aggr(mv[:, q], st6[:, q])
                link(t)
                nc.vector.tensor_scalar(epsv[:], mv[:, :, 1], EPS, None, ALU.add).then_inc(s_var, 1)
                dve.wait_ge(s_rstd, k)
                for q in range(Q):
                    nc.vector.tensor_scalar(dst[:, q], src[:, q], mv[:, q, 0:1], rstd[:, q:q + 1],
                                            ALU.subtract, ALU.mult).then_inc(done, 1)

            def residual(q, count):
                tiles = slice(q, q + count)
                return nc.vector.tensor_tensor(y[:].rearrange("p n (q d) -> p n q d", q=Q)[:, :, tiles],
                                               x1[:].rearrange("p n (q d) -> p n q d", q=Q)[:, :, tiles],
                                               hp[:].rearrange("p q (n d) -> p n q d", n=NH)[:, :, tiles], ALU.add)

            link(statistics(y, 0, 2))
            normalise(y, x1, s_x1, 1, link)
            dve.wait_ge(s_rrc, NB)
            link(nc.vector.tensor_tensor(newrow[:], rrow[:, 1:S + 2], rrow[:, 0:S + 1], ALU.not_equal))
            nc.vector.tensor_scalar(newrow[:], newrow[:], NEG, None, ALU.mult).then_inc(s_new, 1)

            def keep_uv():
                dve.wait_ge(s_h, 2)
                for k in range(2):
                    t = nc.vector.tensor_copy(u_sb[:, 2 * k:2 * k + 2], proj_bank[k][:, :, H:H + 2 * NH])
                t.then_inc(s_uc, 1)
                dve.wait_ge(s_uc, 1)

            steps = [0]

            def slink(ins):
                steps[0] += 1
                ins.then_inc(s_ds, 1)
                dve.wait_ge(s_ds, steps[0])

            with dve.If(sparse == 0):
                keep_uv()
                dve.wait_ge(s_v, 1)
                with dve.Fori(0, Q) as t:
                    at = [0]
                    per = 5 + NH

                    def tlink(ins):
                        at[0] += 1
                        ins.then_inc(s_dd, 1)
                        dve.wait_ge(s_dd, t * per + at[0])

                    u_t = u_sb[:, bass.ds(t, 1), NH:2 * NH].rearrange("p a n -> p (a n)")
                    for n in range(NH):
                        ins = nc.vector.tensor_tensor(vm[:, n], ps_v[n][:].rearrange("p q h -> p (q h)"),
                                                      negm[:, bass.ds(t, 1)].rearrange("p a j -> p (a j)"), ALU.add)
                    tlink(ins)
                    tlink(nc.vector.tensor_reduce(vmax[:], vm, AX, ALU.max))
                    tlink(nc.vector.tensor_tensor(m1[:], vmax[:], u_t, ALU.add))
                    tlink(nc.vector.scalar_tensor_tensor(nmax[:], m1[:], SLOPE, m1[:], ALU.mult, ALU.max))
                    nc.vector.tensor_scalar(nmax[:], nmax[:], -1.0, None, ALU.mult)
                    for n in range(NH):
                        u_tn = u_sb[:, bass.ds(t, 1), NH + n:NH + n + 1].rearrange("p a n -> p (a n)")
                        tlink(nc.vector.tensor_scalar(vm[:, n], vm[:, n], u_tn, None, ALU.add))
                        nc.vector.scalar_tensor_tensor(e_sb[:, n], vm[:, n], SLOPE, vm[:, n], ALU.mult, ALU.max)\
                            .then_inc(s_e, 1)
                    for n in range(NH):
                        dve.wait_ge(s_pt, t * NH + n + 1)
                        nc.vector.tensor_copy(pT[:, n], ps_t[n % 2][:]).then_inc(s_ptc, 1)
                    dve.wait_ge(s_p, t * NH + NH)
                    nc.vector.reciprocal(rinv[:], rsum[:]).then_inc(s_ri, 1)
                    dve.wait_ge(s_ri, t + 1)
                    dve.wait_ge(s_att, t + 1)
                    tlink(nc.vector.tensor_tensor(hp[:, bass.ds(t, 1)].rearrange("p a (n d) -> p (a n) d", n=NH),
                                                  ps_b[:, 0:H].rearrange("p (n d) -> p n d", n=NH),
                                                  rinv[:].unsqueeze(2).broadcast_to([P, NH, D]), ALU.mult))
                slink(residual(0, Q))
                slink(statistics(y, 0, 2))
                normalise(y, out_sb, s_o, 2, slink)
            with dve.Else():
                steps[0] = 0
                keep_uv()
                slink(nc.vector.tensor_copy(uv3[:, :, :, 0], u_sb[:]))
                nc.vector.tensor_tensor(uvres[:], u_sb[:], uv3[:, :, :, 0], ALU.subtract)
                slink(nc.vector.tensor_tensor(uv3[:, :, :, 1], u_sb[:], uv3[:, :, :, 0], ALU.subtract))
                nc.vector.tensor_tensor(uv3[:, :, :, 2], uvres[:], uv3[:, :, :, 1], ALU.subtract).then_inc(s_uv3, 1)
                dve.wait_ge(s_h3, 1)
                for k in range(2):
                    t = nc.vector.tensor_tensor(hres[:, 2 * k:2 * k + 2], proj_bank[k][:, :, 0:H],
                                                h3[:, 0, 2 * k:2 * k + 2], ALU.subtract)
                t.then_inc(s_hres, 1)
                dve.wait_ge(s_h3, 2)
                nc.vector.tensor_tensor(h3[:, 2], hres[:], h3[:, 1], ALU.subtract).then_inc(s_h3, 1)
                dve.wait_ge(s_z, 1)
                slink(nc.vector.tensor_reduce(z_sb[:], z_bank[:, 0:NC * 3 * NH].rearrange("p (c n k) -> p c n k", c=NC, n=NH),
                                              AX, ALU.add))
                nc.vector.scalar_tensor_tensor(z2[:], z_sb[:], SLOPE, z_sb[:], ALU.mult, ALU.max).then_inc(s_zs, 1)
                for b in range(NB):
                    dve.wait_ge(s_zT, b + 1)
                    first = 0.0 if b == 0 else zmax_f[:, b * BS - 1:b * BS]
                    slink(nc.vector.tensor_tensor_scan(zmax_f[:, batch(b)], newrow[:, batch(b)], zT_bank[b][0:NH, 0:BS],
                                                       first, ALU.add, ALU.max))
                nc.vector.tensor_tensor_scan(zmax[:, ::-1], newrow[:, S:0:-1], zmax_f[:, ::-1],
                                             0.0, ALU.add, ALU.max).then_inc(s_zm, 1)
                dve.wait_ge(s_mT, 1)
                nc.vector.tensor_tensor(z_sb[:], z2[:], z_bank[:, 0:NC * NH].rearrange("p (c n) -> p c n", c=NC),
                                        ALU.subtract).then_inc(s_ze, 1)
                dve.wait_ge(s_pe, 1)

                def weigh(b):
                    cs = slice(b * B, (b + 1) * B)
                    nc.vector.tensor_copy(vals[:, cs, H:H + NH], p_edge[:, cs])
                    dve.wait_ge(s_hg, b + 1)
                    nc.vector.tensor_tensor(vals[:, cs, 0:H].rearrange("p c (n d) -> p c n d", n=NH),
                                            hg_bank[b][:, 0:BS].rearrange("p (c n d) -> p c n d", c=B, n=NH),
                                            p_edge[:, cs].unsqueeze(3).broadcast_to([P, B, NH, D]), ALU.mult)\
                        .then_inc(s_vals, 1)

                def residue(b):
                    cs = slice(b * B, (b + 1) * B)
                    dve.wait_ge(s_vhi, b + 1)
                    nc.vector.tensor_tensor(vals[:, cs], vals[:, cs], vals3[:, 0, cs], ALU.subtract).then_inc(s_vres, 1)

                def last_part(b):
                    cs = slice(b * B, (b + 1) * B)
                    dve.wait_ge(s_vmid, b + 1)
                    nc.vector.tensor_tensor(vals3[:, 2, cs], vals[:, cs], vals3[:, 1, cs], ALU.subtract).then_inc(s_v3, 1)

                weigh(0)
                residue(0)
                weigh(1)
                last_part(0)
                residue(1)
                last_part(1)
                weigh(2)
                residue(2)
                last_part(2)

                def reciprocals(k):
                    dve.wait_ge(s_num, k + 1)
                    return nc.vector.reciprocal(dinv[:, 2 * k:2 * k + 2], num_bank[k][:, :, H:H + NH])

                def divide(k):
                    return nc.vector.tensor_tensor(hp[:, 2 * k:2 * k + 2].rearrange("p q (n d) -> p q n d", n=NH),
                                                   num_bank[k][:, :, 0:H].rearrange("p q (n d) -> p q n d", n=NH),
                                                   dinv[:, 2 * k:2 * k + 2].unsqueeze(3).broadcast_to([P, 2, NH, D]),
                                                   ALU.mult)

                slink(reciprocals(0))
                slink(divide(0))
                slink(residual(0, 2))
                reciprocals(1).then_inc(s_rcp, 1)
                statistics(y, 0, 1)
                dve.wait_ge(s_rcp, 1)
                slink(divide(1))
                slink(residual(2, 2))
                slink(statistics(y, 1, 1))
                normalise(y, out_sb, s_o, 2, slink)


_INS = ["x", "adj", "L0_gnn_edge_table", "L0_gnn_w_ih", "L0_gnn_w_hh", "L0_gnn_b_ih", "L0_gnn_b_hh",
        "L1_gnn_W", "L1_gnn_a"]


def kernel(**inputs):
    import numpy as _np
    import concourse.bacc as _bacc
    from concourse import mybir as _mybir
    from concourse.bass_utils import run_bass_kernel_spmd as _run

    nc = _bacc.Bacc("TRN2", target_bir_lowering=False, num_devices=1)
    arrays, args = {}, []
    for name in _INS:
        a = _np.ascontiguousarray(inputs[name])
        arrays[f"in_{name}"] = a
        args.append(nc.dram_tensor(f"in_{name}", a.shape, _mybir.dt.from_np(a.dtype), kind="ExternalInput").ap())
    out = nc.dram_tensor("out_0", inputs["x"].shape, F32, kind="ExternalOutput").ap()
    build_gnn(nc, *args, out)
    r = _run(nc, [arrays], core_ids=[0])
    return r.results[0]["out_0"]
```
